# Optimizing a Trainium2 kernel written in Bass

```python
import numpy as np
import jax
import jax.numpy as jnp

def _softmax(x, axis=-1):
    return jax.nn.softmax(x, axis=axis)

def _gelu(x):
    return jax.nn.gelu(x, approximate=True)

def _silu(x):
    return jax.nn.silu(x)

def _sigmoid(x):
    return jax.nn.sigmoid(x)

def _layernorm(x, axis=-1, eps=1e-05):
    m = jnp.mean(x, axis=axis, keepdims=True)
    v = jnp.var(x, axis=axis, keepdims=True)
    return (x - m) / jnp.sqrt(v + eps)

def _scatter_add(tgt, idx, src, axis=0):
    return tgt.at[idx].add(src)

def _segment_sum(src, seg, n):
    return jax.ops.segment_sum(src, seg, n)
kernel_name = 'mk_flamingo_gated_d2_seqx_r8_63ba83'

def setup_inputs(seed: int=0):
    np.random.seed(seed)
    _w = jnp.asarray

    def _rec_inputs():
        import jax
        import jax.numpy as jnp
        _rk = jax.random.key(seed)
        x = -0.0003929 + 0.9999 * jax.random.normal(jax.random.fold_in(_rk, 1), (64, 64, 128), jnp.float32)
        _lenS = 64 - jax.random.randint(jax.random.fold_in(_rk, 7), (64,), 0, max(1, 64 // 4) + 1, jnp.int32)
        _lenS2 = 64 - jax.random.randint(jax.random.fold_in(_rk, 8), (64,), 0, max(1, 64 // 4) + 1, jnp.int32)
        _ctx_1024P = jax.random.normal(jax.random.fold_in(_rk, 11), (64, 16, 128), jnp.float32)
        _ctx_1024c = jax.random.dirichlet(jax.random.fold_in(_rk, 511), 0.3 * jnp.ones((16,), jnp.float32), (64, 64))
        _ctx_1024t = jnp.einsum('bsk,bkd->bsd', _ctx_1024c, _ctx_1024P)
        _ctx_1024t = _ctx_1024t * jax.lax.rsqrt(jnp.mean(jnp.square(_ctx_1024t)) + 1e-12) * 0.953939
        ctx_1024 = 2.81802e-05 + 1.00001 * (_ctx_1024t + 0.3 * jax.random.normal(jax.random.fold_in(_rk, 611), (64, 64, 128), jnp.float32))
        _g = jax.random.normal(jax.random.fold_in(_rk, 9001), (2, 2), jnp.float32)
        _g = jnp.sign(_g) * jnp.maximum(jnp.abs(_g), 1.0) + (_g == 0) * 1.0
        g_xattn = _g[0]
        g_ffn = _g[1]
        return (x, ctx_1024, g_xattn, g_ffn)
    x, ctx_1024, g_xattn, g_ffn = _rec_inputs()

    def _L0_xattn_setup():
        import jax, jax.numpy as jnp
        import numpy as np
        EMBED_DIM = 128
        N, L = (4, 512)
        key = jax.random.key(seed)
        ks = jax.random.split(key, 9)
        s = 1.0 / np.sqrt(EMBED_DIM)
        return {'q': jax.random.normal(ks[0], (N, L, EMBED_DIM), jnp.float32), 'k': jax.random.normal(ks[1], (N, L, EMBED_DIM), jnp.float32), 'v': jax.random.normal(ks[2], (N, L, EMBED_DIM), jnp.float32), 'Wq': jax.random.normal(ks[3], (EMBED_DIM, EMBED_DIM), jnp.float32) * s, 'bq': jax.random.normal(ks[4], (EMBED_DIM,), jnp.float32) * s, 'Wk': jax.random.normal(ks[5], (EMBED_DIM, EMBED_DIM), jnp.float32) * s, 'bk': jax.random.normal(ks[6], (EMBED_DIM,), jnp.float32) * s, 'Wv': jax.random.normal(ks[7], (EMBED_DIM, EMBED_DIM), jnp.float32) * s, 'bv': jax.random.normal(ks[8], (EMBED_DIM,), jnp.float32) * s}
    _L0_xattn_all = _L0_xattn_setup()
    _L0_xattn_in = {k: v for k, v in _L0_xattn_all.items() if k in ('Wq', 'bq', 'Wk', 'bk', 'Wv', 'bv')}
    del _L0_xattn_all

    def _L0_ffn_setup():
        import jax, jax.numpy as jnp
        import numpy as np
        E, D, F = (8, 128, 512)
        LN_EPS = 1e-05
        key = jax.random.key(seed)
        k = jax.random.split(key, 8)
        x = jax.random.normal(k[0], (4, 256, D), jnp.float32)
        centroids = jax.random.normal(k[1], (E, D), jnp.float32) * 0.1
        ln_g = jnp.ones((E, D), jnp.float32)
        ln_b = jnp.zeros((E, D), jnp.float32)
        w1 = jax.random.normal(k[2], (E, F, D), jnp.float32) * (1.0 / np.sqrt(D))
        b1 = jnp.zeros((E, F), jnp.float32)
        w2 = jax.random.normal(k[3], (E, D, F), jnp.float32) * (1.0 / np.sqrt(F))
        b2 = jnp.zeros((E, D), jnp.float32)
        return {'input_features': x, 'centroids': centroids, 'ln_g': ln_g, 'ln_b': ln_b, 'w1': w1, 'b1': b1, 'w2': w2, 'b2': b2}
    _L0_ffn_all = _L0_ffn_setup()
    _L0_ffn_in = {k: v for k, v in _L0_ffn_all.items() if k in ('centroids', 'ln_g', 'ln_b', 'w1', 'b1', 'w2', 'b2')}
    del _L0_ffn_all

    def _L1_xattn_setup():
        import jax, jax.numpy as jnp
        import numpy as np
        B, S, C = (8, 256, 128)
        key = jax.random.key(seed)
        ks = jax.random.split(key, 9)
        scale = 1.0 / np.sqrt(C)
        return {'x1': jax.random.normal(ks[0], (B, S, C), jnp.float32), 'x2': jax.random.normal(ks[1], (B, S, C), jnp.float32), 'x3': jax.random.normal(ks[2], (B, S, C), jnp.float32), 'Wq': jax.random.normal(ks[3], (C, C), jnp.float32) * scale, 'bq': jax.random.normal(ks[4], (C,), jnp.float32) * scale, 'Wk': jax.random.normal(ks[5], (C, C), jnp.float32) * scale, 'bk': jax.random.normal(ks[6], (C,), jnp.float32) * scale, 'Wv': jax.random.normal(ks[7], (C, C), jnp.float32) * scale, 'bv': jax.random.normal(ks[8], (C,), jnp.float32) * scale}
    _L1_xattn_all = _L1_xattn_setup()
    _L1_xattn_in = {k: v for k, v in _L1_xattn_all.items() if k in ('Wq', 'bq', 'Wk', 'bk', 'Wv', 'bv')}
    del _L1_xattn_all

    def _L1_ffn_setup():
        import jax, jax.numpy as jnp
        import numpy as np
        NUM_EXPERTS = 8
        IN_FEATURES = 128
        HIDDEN_FEATURES = 512
        GATE_DIM = 16
        EPS = 0.0001
        key = jax.random.key(seed)
        ks = jax.random.split(key, 7)
        hidden_states = jax.random.normal(ks[0], (1, 256, IN_FEATURES), dtype=jnp.float32)
        wg_red = jax.random.normal(ks[1], (GATE_DIM, IN_FEATURES), dtype=jnp.float32) * 0.02
        wg = jax.random.normal(ks[2], (NUM_EXPERTS, GATE_DIM), dtype=jnp.float32)
        w1 = jax.random.uniform(ks[3], (NUM_EXPERTS, IN_FEATURES, HIDDEN_FEATURES), dtype=jnp.float32)
        b1 = jax.random.uniform(ks[4], (NUM_EXPERTS, HIDDEN_FEATURES), dtype=jnp.float32)
        w2 = jax.random.uniform(ks[5], (NUM_EXPERTS, HIDDEN_FEATURES, IN_FEATURES), dtype=jnp.float32)
        b2 = jax.random.uniform(ks[6], (NUM_EXPERTS, IN_FEATURES), dtype=jnp.float32)
        return {'hidden_states': hidden_states, 'wg_red': wg_red, 'wg': wg, 'w1': w1, 'b1': b1, 'w2': w2, 'b2': b2}
    _L1_ffn_all = _L1_ffn_setup()
    _L1_ffn_in = {k: v for k, v in _L1_ffn_all.items() if k in ('wg_red', 'wg', 'w1', 'b1', 'w2', 'b2')}
    del _L1_ffn_all
    return {'x': x, 'ctx_1024': ctx_1024, 'g_xattn': g_xattn, 'g_ffn': g_ffn, 'L0_xattn_Wq': _L0_xattn_in['Wq'], 'L0_xattn_bq': _L0_xattn_in['bq'], 'L0_xattn_Wk': _L0_xattn_in['Wk'], 'L0_xattn_bk': _L0_xattn_in['bk'], 'L0_xattn_Wv': _L0_xattn_in['Wv'], 'L0_xattn_bv': _L0_xattn_in['bv'], 'L0_ffn_centroids': _L0_ffn_in['centroids'], 'L0_ffn_ln_g': _L0_ffn_in['ln_g'], 'L0_ffn_ln_b': _L0_ffn_in['ln_b'], 'L0_ffn_w1': _L0_ffn_in['w1'], 'L0_ffn_b1': _L0_ffn_in['b1'], 'L0_ffn_w2': _L0_ffn_in['w2'], 'L0_ffn_b2': _L0_ffn_in['b2'], 'L1_xattn_Wq': _L1_xattn_in['Wq'], 'L1_xattn_bq': _L1_xattn_in['bq'], 'L1_xattn_Wk': _L1_xattn_in['Wk'], 'L1_xattn_bk': _L1_xattn_in['bk'], 'L1_xattn_Wv': _L1_xattn_in['Wv'], 'L1_xattn_bv': _L1_xattn_in['bv'], 'L1_ffn_wg_red': _L1_ffn_in['wg_red'], 'L1_ffn_wg': _L1_ffn_in['wg'], 'L1_ffn_w1': _L1_ffn_in['w1'], 'L1_ffn_b1': _L1_ffn_in['b1'], 'L1_ffn_w2': _L1_ffn_in['w2'], 'L1_ffn_b2': _L1_ffn_in['b2']}

def reference(x, ctx_1024, g_xattn, g_ffn, L0_xattn_Wq, L0_xattn_bq, L0_xattn_Wk, L0_xattn_bk, L0_xattn_Wv, L0_xattn_bv, L0_ffn_centroids, L0_ffn_ln_g, L0_ffn_ln_b, L0_ffn_w1, L0_ffn_b1, L0_ffn_w2, L0_ffn_b2, L1_xattn_Wq, L1_xattn_bq, L1_xattn_Wk, L1_xattn_bk, L1_xattn_Wv, L1_xattn_bv, L1_ffn_wg_red, L1_ffn_wg, L1_ffn_w1, L1_ffn_b1, L1_ffn_w2, L1_ffn_b2):
    import jax
    import jax.numpy as jnp

    def _L0_xattn_ref(q, k, v, Wq, bq, Wk, bk, Wv, bv):
        import jax, jax.numpy as jnp
        import numpy as np
        EMBED_DIM = 128
        N, L = (4, 512)
        scale = 1.0 / q.shape[-1] ** 0.5
        pq = jnp.einsum('nle,fe->nlf', q, Wq) + bq
        pk = jnp.einsum('nle,fe->nlf', k, Wk) + bk
        pv = jnp.einsum('nle,fe->nlf', v, Wv) + bv
        scores = jnp.einsum('nle,nme->nlm', pq, pk) * scale
        attn = jax.nn.softmax(scores, axis=-1)
        return jnp.einsum('nlm,nme->nle', attn, pv)

    def _L0_ffn_ref(input_features, centroids, ln_g, ln_b, w1, b1, w2, b2):
        import jax, jax.numpy as jnp
        import numpy as np
        E, D, F = (8, 128, 512)
        LN_EPS = 1e-05
        x = input_features.reshape(-1, D)
        aff = jax.lax.stop_gradient(x) @ centroids.T
        assign = jnp.argmax(aff, axis=1)
        onehot = jax.nn.one_hot(assign, E, dtype=x.dtype)
        mu = jnp.mean(x, axis=-1, keepdims=True)
        var = jnp.mean((x - mu) ** 2, axis=-1, keepdims=True)
        xhat = (x - mu) * jax.lax.rsqrt(var + LN_EPS)
        xn = xhat[None, :, :] * ln_g[:, None, :] + ln_b[:, None, :]
        h = jax.nn.relu(jnp.einsum('etd,efd->etf', xn, w1) + b1[:, None, :])
        y = x[None, :, :] + jnp.einsum('etf,edf->etd', h, w2) + b2[:, None, :]
        alpha = jax.nn.sigmoid(x @ centroids.T)
        a = alpha.T[:, :, None]
        gated = a * y + (1.0 - a) * x[None, :, :]
        out = jnp.einsum('te,etd->td', onehot, gated)
        return out.reshape(input_features.shape)

    def _L1_xattn_ref(x1, x2, x3, Wq, bq, Wk, bk, Wv, bv):
        import jax, jax.numpy as jnp
        import numpy as np
        B, S, C = (8, 256, 128)
        q = jnp.einsum('bsc,dc->bsd', x1, Wq) + bq
        k = jnp.einsum('bsc,dc->bsd', x2, Wk) + bk
        v = jnp.einsum('bsc,dc->bsd', x3, Wv) + bv
        scores = jnp.einsum('bqd,bkd->bqk', q, k)
        attn = jax.nn.softmax(scores, axis=-1)
        return jnp.einsum('bqk,bkd->bqd', attn, v)

    def _L1_ffn_ref(hidden_states, wg_red, wg, w1, b1, w2, b2):
        import jax, jax.numpy as jnp
        import numpy as np
        NUM_EXPERTS = 8
        IN_FEATURES = 128
        HIDDEN_FEATURES = 512
        GATE_DIM = 16
        EPS = 0.0001
        b, t, c = hidden_states.shape
        x = hidden_states.reshape(-1, c)
        xr = x @ wg_red.T
        wg_unit = wg / jnp.maximum(jnp.linalg.norm(wg, axis=1, keepdims=True), EPS)
        logits = xr @ wg_unit.T
        gates = jax.nn.softmax(logits, axis=1)
        indices_s = jnp.argmax(gates, axis=1)
        scores = jnp.max(gates, axis=1)
        E = wg.shape[0]
        out = jnp.zeros_like(x)
        for e in range(E):
            mask = (indices_s == e).astype(x.dtype)[:, None]
            h = jax.nn.gelu(x @ w1[e] + b1[e], approximate=False)
            out = out + mask * (h @ w2[e] + b2[e])
        out = out * scores[:, None]
        return out.reshape(b, t, c)
    x = x + jnp.tanh(g_xattn[0]) * _L0_xattn_ref(_layernorm(x, axis=-1), ctx_1024, ctx_1024, L0_xattn_Wq, L0_xattn_bq, L0_xattn_Wk, L0_xattn_bk, L0_xattn_Wv, L0_xattn_bv)
    x = x + jnp.tanh(g_ffn[0]) * _L0_ffn_ref(_layernorm(x, axis=-1), L0_ffn_centroids, L0_ffn_ln_g, L0_ffn_ln_b, L0_ffn_w1, L0_ffn_b1, L0_ffn_w2, L0_ffn_b2)
    x = x + jnp.tanh(g_xattn[1]) * _L1_xattn_ref(_layernorm(x, axis=-1), ctx_1024, ctx_1024, L1_xattn_Wq, L1_xattn_bq, L1_xattn_Wk, L1_xattn_bk, L1_xattn_Wv, L1_xattn_bv)
    x = x + jnp.tanh(g_ffn[1]) * _L1_ffn_ref(_layernorm(x, axis=-1), L1_ffn_wg_red, L1_ffn_wg, L1_ffn_w1, L1_ffn_b1, L1_ffn_w2, L1_ffn_b2)
    return x

_drawn_inputs = setup_inputs


def setup_inputs(seed=0):
    import zlib

    import numpy as np

    out = dict(_drawn_inputs(seed))
    spreads = {'g_ffn': (-1.0, 0.2),
     'L0_ffn_ln_g': (1.0, 0.2),
     'L0_ffn_ln_b': (0.0, 0.1),
     'L0_ffn_b1': (0.0, 0.1),
     'L0_ffn_b2': (0.0, 0.1)}
    factors = {'L0_xattn_bq': 2.682,
     'L0_xattn_bk': 64.0,
     'L1_xattn_bk': 64.0,
     'L1_ffn_b1': 8.0,
     'L1_ffn_b2': 64.0,
     'L1_xattn_bv': 2.786}
    for name, (base, spread) in spreads.items():
        noise = np.random.default_rng([zlib.crc32(name.encode()), seed]).standard_normal(out[name].shape)
        drawn = base * np.exp(spread * noise) if base else spread * noise
        out[name] = jnp.asarray(drawn.astype(out[name].dtype))
    for name, factor in factors.items():
        out[name] = (out[name] * factor).astype(out[name].dtype)
    return out
```

```python
from contextlib import ExitStack

import concourse.bass as bass
from concourse import mybir

F32 = mybir.dt.float32
I32 = mybir.dt.int32
ALU = mybir.AluOpType
ACT = mybir.ActivationFunctionType
X_AXIS = mybir.AxisListType.X

P = 128
EPS = 1e-5
GATE_EPS = 1e-4
EMPTY = 8192.0


def build(nc, t, out):
    B, S, D = t["x"].shape
    E, F, _ = t["L0_ffn_w1"].shape
    R = t["L1_ffn_wg_red"].shape[0]
    TOK = B * S
    TILES = TOK // P
    GT = 4
    G = TILES // GT
    W = GT * D
    FC = F // P
    ST = TILES + E - 1
    RW = 2 * D + 4
    assert D == P and S * 2 == P and ST % 3 == 0 and P // 2 == S

    x_rows = t["x"].rearrange("b s d -> (b s) d")
    ctx_rows = t["ctx_1024"].rearrange("b s d -> (b s) d")
    out_rows = out.rearrange("b s d -> (b s) d")
    tok_rows = [nc.dram_tensor("tok_rows0", [TOK, D], F32, kind="Internal").ap(),
                nc.dram_tensor("tok_rows1", [TOK, RW], F32, kind="Internal").ap()]
    mlp_rows = nc.dram_tensor("mlp_rows", [ST * P, D], F32, kind="Internal").ap()

    with ExitStack() as ctx:
        def sb(name, shape, dt=F32):
            return ctx.enter_context(nc.sbuf_tensor(name, shape, dt))

        def sem(name):
            return ctx.enter_context(nc.semaphore(name))

        X = sb("X", [P, TOK])
        ctxT = sb("ctxT", [P, TOK])
        WT = [[sb(f"WT{l}{m}", [P, D]) for m in "qkv"] for l in range(2)]
        bias_qk = sb("bias_qk", [P, 4])
        bias_v = sb("bias_v", [P, 2, D])
        W1 = [sb(f"W1_{l}", [P, E * F]) for l in range(2)]
        W2 = [sb(f"W2_{l}", [P, E * F]) for l in range(2)]
        B1 = sb("B1", [P, E * F])
        B2 = [sb(f"B2_{l}", [P, E * D]) for l in range(2)]
        ln_gT, ln_bT = sb("ln_gT", [P, E]), sb("ln_bT", [P, E])
        gateT = [sb("gateT0", [P, E]), sb("gateT1", [P, E])]
        tanh_g = sb("tanh_g", [P, 4])
        ident, ones = sb("ident", [P, P]), sb("ones", [P, P])
        before = sb("before", [P, P])
        iota_e = sb("iota_e", [P, E])
        iota_p = sb("iota_p", [P, P])
        iota_s = sb("iota_s", [P, ST])
        token1 = sb("token1", [P, TILES])
        eps_c, one_c = sb("eps_c", [P, 1]), sb("one_c", [P, 1])

        raw_small = sb("raw_small", [E, 3, D])
        wg_raw, wg_red = sb("wg_raw", [E, R]), sb("wg_red", [R, D])
        wg_sq, wg_ss, wg_ln = sb("wg_sq", [E, R]), sb("wg_ss", [E, 1]), sb("wg_ln", [E, 1])
        wg_r, wg_t, wg_u = sb("wg_r", [E, 1]), sb("wg_t", [E, 3]), sb("wg_u", [E, R])
        wg_uT = sb("wg_uT", [R, E])
        graw = sb("graw", [P, 4])

        ctx_raw = [sb(f"ctx_raw{i}", [P, GT, D]) for i in range(2)]
        xn = [sb(f"xn{i}", [P, GT, D]) for i in range(2)]
        xnT = [sb(f"xnT{i}", [P, W]) for i in range(2)]
        qT = [sb(f"qT{i}", [P, W]) for i in range(2)]
        kT = [sb(f"kT{i}", [P, W]) for i in range(2)]
        v = [sb(f"v{i}", [P, GT, D]) for i in range(2)]
        sc = [sb(f"sc{i}", [P, GT, S]) for i in range(2)]
        pr = [sb(f"pr{i}", [P, GT, S]) for i in range(2)]
        prn = [sb(f"prn{i}", [P, GT, S]) for i in range(2)]
        prT = [sb(f"prT{i}", [P, GT, P]) for i in range(2)]
        xn2 = [sb(f"xn2{i}", [P, GT, D]) for i in range(2)]
        xn2T = [sb(f"xn2T{i}", [P, W]) for i in range(2)]
        hat = [sb(f"hat{i}", [P, GT, RW]) for i in range(2)]
        bn6 = sb("bn6", [P, GT, 6])
        mvA = [sb(f"mvA{i}", [P, GT, 2]) for i in range(2)]
        mvB = [sb(f"mvB{i}", [P, GT, 2]) for i in range(2)]
        vC = [sb(f"vC{i}", [P, GT]) for i in range(2)]
        lnr = {k: [sb(f"ln{k}{i}", [P, GT]) for i in range(2)] for k in "ABC"}
        r0 = {k: [sb(f"r0{k}{i}", [P, GT]) for i in range(2)] for k in "ABC"}
        rs = {k: [sb(f"rs{k}{i}", [P, GT]) for i in range(2)] for k in "ABC"}
        nt = sb("nt", [P, 3, GT])
        mx, den, rden = sb("mx", [P, GT]), sb("den", [P, GT]), sb("rden", [P, GT])
        rdg = [sb(f"rdg{i}", [P, GT]) for i in range(2)]
        ymlp = [sb(f"ymlp{i}", [P, W]) for i in range(2)]

        LG = sb("LG", [P, TILES, E])
        top = sb("top", [P, TILES])
        alpha = sb("alpha", [P, TILES])
        gl, gs = sb("gl", [P, GT, E]), sb("gs", [P, GT, E])
        gm, gd = sb("gm", [P, GT]), sb("gd", [P, GT])
        hit = sb("hit", [P, TILES, E])
        first = sb("first", [P, TILES])
        oh = sb("oh", [P, E, TILES])
        cum = sb("cum", [P, E, TILES])
        ones_et = sb("ones_et", [P, E * TILES])
        cnt, ends = sb("cnt", [P, E]), sb("ends", [P, E])
        tf, ti = sb("tf", [P, E]), sb("ti", [P, E], I32)
        tcnt, tend, off = sb("tcnt", [P, E]), sb("tend", [P, E]), sb("off", [P, E])
        slot_f = sb("slot_f", [P, TILES])
        slot = sb("slot", [P, TILES], I32)
        hi_i, lo_i = sb("hi_i", [P, TILES], I32), sb("lo_i", [P, TILES], I32)
        hi, lo = sb("hi", [P, TILES]), sb("lo", [P, TILES])
        in_lo = [sb(f"in_lo{i}", [P, P]) for i in range(4)]
        in_hi = [sb(f"in_hi{i}", [P, ST]) for i in range(4)]
        ge = sb("ge", [P, ST, E])
        eid_f, eid = sb("eid_f", [P, ST]), sb("eid", [P, ST], I32)
        inv_f, src_f, dst_f = sb("inv_f", [P, ST]), sb("src_f", [P, ST]), sb("dst_f", [P, ST])
        src, dst = sb("src", [P, ST], I32), sb("dst", [P, ST], I32)

        rows = [b[:, :, :].rearrange("p j d -> p (j d)") for b in (*v, *xn, *xn2)]
        rT = [sb(f"rT{i}", [P, P]) for i in range(3)]
        hb = [qT[0], qT[1], kT[0]]
        hT = [kT[1], xnT[0], xnT[1]]
        yb = [sb(f"yb{i}", [P, D]) for i in range(3)]
        ob = [sb(f"ob{i}", [P, D]) for i in range(3)]

        bank = [ctx.enter_context(nc.psum_tensor(f"bank{i}", [P, 512], F32)) for i in range(8)]
        pC, pS, pT, pK, pV, pP, pQ, pO = bank
        pL = pS[:, GT * S:GT * S + GT * E]
        pX, pH, pHT, pY = bank[0], bank[1:4], bank[4:7], bank[7]

        s_const = sem("s_const")
        s_wload = [sem(f"s_wload{i}") for i in range(5)]
        s_small = sem("s_small")
        s_l1w = sem("s_l1w")
        s_wt = sem("s_wt")
        s_wtc = sem("s_wtc")
        s_gate = sem("s_gate")
        s_tanh = sem("s_tanh")
        s_in = [sem(f"s_in{i}") for i in range(2)]
        s_cT, s_cTc = sem("s_cT"), sem("s_cTc")
        s_stA, s_r0A, s_rsA = sem("s_stA"), sem("s_r0A"), sem("s_rsA")
        s_stB, s_r0B, s_rsB = sem("s_stB"), sem("s_r0B"), sem("s_rsB")
        s_vC, s_r0C, s_rsC = sem("s_vC"), sem("s_r0C"), sem("s_rsC")
        s_xn, s_xT, s_xTc = sem("s_xn"), sem("s_xT"), sem("s_xTc")
        s_q, s_qc, s_k, s_kc, s_v, s_vc = (sem(n) for n in ("s_q", "s_qc", "s_k", "s_kc", "s_v", "s_vc"))
        s_sc, s_sub, s_exp, s_rd, s_prn = (sem(n) for n in ("s_sc", "s_sub", "s_exp", "s_rd", "s_prn"))
        s_pT, s_pTc, s_pv, s_x1 = (sem(n) for n in ("s_pT", "s_pTc", "s_pv", "s_x1"))
        s_xn2, s_x2T, s_x2Tc, s_lg, s_lgc = (sem(n) for n in ("s_xn2", "s_x2T", "s_x2Tc", "s_lg", "s_lgc"))
        s_gsub, s_gexp, s_row, s_rowp = sem("s_gsub"), sem("s_gexp"), sem("s_row"), sem("s_rowp")
        s_store = [sem(f"s_store{i}") for i in range(2)]
        s_yback = [sem(f"s_yback{i}") for i in range(2)]
        s_x2 = sem("s_x2")
        s_dve = sem("s_dve")
        s_act = sem("s_act")
        s_cnt, s_pfx, s_hilo, s_lo, s_hi, s_invm, s_src, s_eid = (
            sem(n) for n in ("s_cnt", "s_pfx", "s_hilo", "s_lo", "s_hi", "s_invm", "s_src", "s_eid"))
        s_aexp, s_azs = sem("s_aexp"), sem("s_azs")
        s_row_in = [[sem(f"s_row_in{l}{i}") for i in range(6)] for l in range(2)]
        s_rt, s_rtc, s_h, s_hb, s_ht, s_hTc, s_y, s_yb = (
            sem(n) for n in ("s_rt", "s_rtc", "s_h", "s_hb", "s_ht", "s_hTc", "s_y", "s_yb"))
        s_out = [sem(f"s_out{i}") for i in range(3)]
        s_scat = [sem(f"s_scat{i}") for i in range(3)]
        s_y1 = sem("s_y1")
        N_CONST = 11

        block = ctx.enter_context(nc.Block())

        def n(l, g):
            return l * G + g + 1

        def cols(g):
            return slice(g * W, (g + 1) * W)

        def tiles3(ap):
            return ap.rearrange("p (j d) -> p j d", j=GT)

        def each_step(l, step):
            for i in range(-2, G + 1):
                step(i)

        U = 6

        def each_tile(eng, lead, tail, step):
            for s in range(-lead, U):
                step(s // U, s % U)
            with eng.Fori(1, ST // U) as q:
                for r in range(U):
                    step(q, r)
            for s in range(ST // U * U, ST + tail):
                step(s // U, s % U)

        def ahead(q, r, k):
            return q + (r + k) // U, (r + k) % U

        def num(q, r):
            return U * q + r

        def third(q, r):
            return U // 3 * q + r // 3

        def valid(q, r):
            return not isinstance(q, int) or 0 <= num(q, r) < ST

        def has_before(l, q, r, k):
            return l == 1 or not isinstance(q, int) or num(q, r) >= k

        @block.sync
        def _(sp):
            def load_group(g):
                for dst_ap, rows_ap in ((tiles3(X[:, cols(g)]), x_rows), (ctx_raw[g % 2][:, :, :], ctx_rows)):
                    sp.dma_start(dst_ap, rows_ap[g * GT * P:(g + 1) * GT * P, :].rearrange("(j p) d -> p j d", p=P)
                                 ).then_inc(s_in[g % 2], 16)

            load_group(0)
            sp.dma_start(graw[:, 0:2], t["g_xattn"].partition_broadcast(P)).then_inc(s_small, 16)
            sp.dma_start(graw[:, 2:4], t["g_ffn"].partition_broadcast(P)).then_inc(s_small, 16)
            for l in range(2):
                for m in range(2):
                    sp.dma_start(bias_qk[:, 2 * l + m:2 * l + m + 1],
                                 t[f"L{l}_xattn_b{'qk'[m]}"].rearrange("(p o) -> p o", o=1)).then_inc(s_small, 16)
                sp.dma_start(bias_v[:, l, :], t[f"L{l}_xattn_bv"].partition_broadcast(P)).then_inc(s_small, 16)
            for m, name in enumerate(("centroids", "ln_g", "ln_b")):
                sp.dma_start(raw_small[:, m, :], t[f"L0_ffn_{name}"]).then_inc(s_small, 16)
            sp.dma_start(wg_raw[:, :], t["L1_ffn_wg"]).then_inc(s_small, 16)
            sp.dma_start(wg_red[:, :], t["L1_ffn_wg_red"]).then_inc(s_small, 16)
            load_group(1)
            sp.dma_start(W1[1][:, :].rearrange("p (e c d) -> p e c d", e=E, c=FC),
                         t["L0_ffn_w1"].rearrange("e (c p) d -> p e c d", p=P)).then_inc(s_wload[1], 16)
            sp.dma_start(W2[1][:, :].rearrange("p (e f) -> p e f", e=E),
                         t["L0_ffn_w2"].rearrange("e p f -> p e f")).then_inc(s_wload[2], 16)
            sp.dma_start(B1[:, :], t["L0_ffn_b1"].rearrange("e f -> (e f)").partition_broadcast(P)
                         ).then_inc(s_wload[3], 16)
            for l in range(2):
                sp.dma_start(B2[l][:, :], t[f"L{l}_ffn_b2"].rearrange("e d -> (e d)").partition_broadcast(P)
                             ).then_inc(s_wload[3], 16)

            def store_rows(l, g):
                sp.wait_ge(s_rowp, n(l, g))
                if l == 1:
                    sp.wait_ge(s_row, g + 1)
                wide = (D, RW)[l]
                sp.dma_start(tok_rows[l][g * GT * P:(g + 1) * GT * P, :].rearrange("(j p) d -> p j d", p=P),
                             hat[g % 2][:, :, 0:wide]).then_inc(s_store[g % 2], 16)

            for g in range(2, G + 4):
                if g < G:
                    sp.wait_ge(s_cT, g - 1)
                    load_group(g)
                if g >= 4:
                    store_rows(0, g - 4)
            sp.wait_ge(s_wt, 2 + 2 * E)
            sp.dma_start(W1[1][:, :].rearrange("p (e f) -> p e f", e=E),
                         t["L1_ffn_w1"].rearrange("e d f -> d e f")).then_inc(s_l1w, 16)
            sp.dma_start(W2[1][:, :].rearrange("p (e c d) -> p e c d", e=E, c=FC),
                         t["L1_ffn_w2"].rearrange("e (c p) d -> p e c d", p=P)).then_inc(s_l1w, 16)

            def store_mlp(q, r):
                q, r = ahead(q, r, -1)
                if not valid(q, r):
                    return
                sp.wait_ge(s_yb, num(q, r) + 1)
                sp.dma_start(mlp_rows[bass.ds((num(q, r)) * P, P), :], yb[r % 3][:, :]).then_inc(s_out[r % 3], 16)

            each_tile(sp, 0, 1, store_mlp)
            sp.wait_ge(s_hb, ST)
            sp.dma_start(B1[:, :], t["L1_ffn_b1"].rearrange("e f -> (e f)").partition_broadcast(P)
                         ).then_inc(s_wload[3], 16)
            for g in range(G):
                store_rows(1, g)
            for r in range(3):
                sp.wait_ge(s_scat[r], 16 * (ST // 3))

        @block.gpsimd
        def _(pool):
            pool.memset(ident[:, :], 0.0).then_inc(s_const, 1)
            pool.memset(before[:, :], 1.0).then_inc(s_const, 1)
            pool.memset(ones[:, :], 1.0).then_inc(s_const, 1)
            pool.iota(iota_e[:, :], [[1, E]], base=-E, channel_multiplier=0,
                      allow_small_or_imprecise_dtypes=True).then_inc(s_const, 1)
            pool.iota(iota_p[:, :], [[1, P]], base=0, channel_multiplier=0,
                      allow_small_or_imprecise_dtypes=True).then_inc(s_const, 1)
            pool.iota(iota_s[:, :], [[1, ST]], base=0, channel_multiplier=0,
                      allow_small_or_imprecise_dtypes=True).then_inc(s_const, 1)
            pool.iota(token1[:, :], [[P, TILES]], base=1, channel_multiplier=1,
                      allow_small_or_imprecise_dtypes=True).then_inc(s_const, 1)
            pool.memset(ones_et[:, :], 1.0).then_inc(s_const, 1)
            pool.wait_ge(s_const, 8)
            pool.affine_select(out=ident[:, :], in_=ident[:, :], compare_op=ALU.not_equal, fill=1.0, base=0,
                               pattern=[[-1, P]], channel_multiplier=1).then_inc(s_const, 1)
            pool.affine_select(out=before[:, :], in_=before[:, :], compare_op=ALU.is_gt, fill=0.0, base=0,
                               pattern=[[1, P]], channel_multiplier=-1).then_inc(s_const, 1)
            pool.memset(prT[0][:, :, :], 0.0)
            pool.memset(hat[0][:, :, :], 0.0)
            pool.memset(hat[1][:, :, :], 0.0)
            pool.memset(prT[1][:, :, :], 0.0).then_inc(s_const, 1)

            def xn_tiles(l, g):
                pool.wait_ge(s_rsA, n(l, g))
                if l == 0:
                    pool.wait_ge(s_in[g % 2], 32 * (g // 2 + 1))
                if n(l, g) > 2:
                    pool.wait_ge(s_xT, n(l, g) - 2)
                for j in range(GT):
                    ins = pool.tensor_scalar(xn[g % 2][:, j, :], X[:, g * W + j * D:g * W + (j + 1) * D],
                                             mvA[g % 2][:, j, 0:1], rs["A"][g % 2][:, j:j + 1],
                                             ALU.subtract, ALU.mult)
                ins.then_inc(s_xn, 1)

            def norm_probs(l, g):
                pool.wait_ge(s_exp, n(l, g))
                pool.wait_ge(s_rd, n(l, g))
                if n(l, g) > 2:
                    pool.wait_ge(s_pT, n(l, g) - 2)
                pool.tensor_tensor(prn[g % 2][:, :, :], pr[g % 2][:, :, :],
                                   rdg[g % 2][:, :].unsqueeze(2).to_broadcast([P, GT, S]), ALU.mult
                                   ).then_inc(s_prn, 1)

            def xn2_tiles(l, g):
                pool.wait_ge(s_rsB, n(l, g))
                if n(l, g) > 2:
                    pool.wait_ge(s_x2T, n(l, g) - 2)
                    pool.wait_ge(s_x2, min(G, n(l, g) - 2))
                if l == 1 or g >= 2:
                    pool.wait_ge(s_store[g % 2], 16 * (l * (G // 2) + g // 2))
                for j in range(GT):
                    ins = pool.tensor_scalar(xn2[g % 2][:, j, :], X[:, g * W + j * D:g * W + (j + 1) * D],
                                             mvB[g % 2][:, j, 0:1], rs["B"][g % 2][:, j:j + 1],
                                             ALU.subtract, ALU.mult)
                ins.then_inc(s_xn2, 1)
                pool.wait_ge(s_xn2, n(l, g))
                if l == 0:
                    pool.wait_ge(s_rsC, g + 1)
                    for j in range(GT):
                        ins = pool.tensor_scalar(hat[g % 2][:, j, 0:D], xn2[g % 2][:, j, :],
                                                 rs["C"][g % 2][:, j:j + 1], None, ALU.mult)
                else:
                    pool.tensor_copy(hat[g % 2][:, :, 0:D], xn2[g % 2][:, :, :])
                    ins = pool.tensor_copy(hat[g % 2][:, :, D:2 * D], tiles3(X[:, cols(g)]))
                ins.then_inc(s_rowp, 1)

            def gather_back(g):
                if g >= 2:
                    pool.wait_ge(s_stA, n(1, g - 2))
                for j in range(GT):
                    pool.indirect_dma_start(ymlp[g % 2][:, j * D:(j + 1) * D], None, mlp_rows,
                                            bass.IndirectOffsetOnAxis(ap=slot[:, g * GT + j:g * GT + j + 1], axis=0),
                                            bounds_check=ST * P - 1, oob_is_err=False
                                            ).then_inc(s_yback[g % 2], 16)

            def attention(l):
                def step(i):
                    if l == 1 and i + 4 < G and i >= -2:
                        gather_back(i + 4)
                    if 0 <= i - 1 < G:
                        xn2_tiles(l, i - 1)
                    if 0 <= i < G:
                        norm_probs(l, i)
                    if 0 <= i + 2 < G:
                        xn_tiles(l, i + 2)
                each_step(l, step)

            def in_tile(l):
                for tt in range(TILES):
                    pool.wait_ge(s_hilo, l + 1)
                    if l * TILES + tt >= 4:
                        pool.wait_ge(s_invm, l * TILES + tt - 3)
                    pool.tensor_scalar(in_hi[tt % 4][:, :], iota_s[:, :], hi[:, tt:tt + 1], token1[:, tt:tt + 1],
                                       ALU.is_equal, ALU.mult).then_inc(s_hi, 1)

            def gather(l, s):
                if s >= 6:
                    pool.wait_ge(s_rt if l == 0 else s_yb, l * ST + s - 5)
                pool.indirect_dma_start(rows[s % 6][:, 0:(D, RW)[l]], None, tok_rows[l],
                                        bass.IndirectOffsetOnAxis(ap=src[:, s:s + 1], axis=0),
                                        bounds_check=TOK - 1, oob_is_err=False).then_inc(s_row_in[l][s % 6], 16)

            def scatter(s):
                pool.wait_ge(s_yb, ST + s + 1)
                pool.indirect_dma_start(out_rows, bass.IndirectOffsetOnAxis(ap=dst[:, s:s + 1], axis=0),
                                        ob[s % 3][:, :], None,
                                        bounds_check=TOK - 1, oob_is_err=False).then_inc(s_scat[s % 3], 16)

            for l in range(2):
                attention(l)
                in_tile(l)
                pool.wait_ge(s_src, l + 1)
                for h in range(2):
                    pool.wait_ge(s_store[h], 16 * (l + 1) * (G // 2))
                for s in range(ST + 4):
                    if s < ST:
                        gather(l, s)
                    if l == 1 and s >= 4:
                        scatter(s - 4)
                if l == 0:
                    for r in range(3):
                        pool.wait_ge(s_out[r], 16 * (ST // 3))
                    gather_back(0)
                    gather_back(1)

        @block.scalar
        def _(act):
            act.dma_start(WT[0][0][:, :], t["L0_xattn_Wq"]).then_inc(s_wload[0], 16)
            act.dma_start(WT[0][1][:, :], t["L0_xattn_Wk"]).then_inc(s_wload[0], 16)
            act.dma_start(WT[0][2][:, :], t["L0_xattn_Wv"]).then_inc(s_wload[0], 16)
            for m in range(3):
                act.dma_start(WT[1][m][:, :], t[f"L1_xattn_W{'qkv'[m]}"]).then_inc(s_wload[0], 16)
            chain = [0]

            def link(ins):
                chain[0] += 1
                ins.then_inc(s_act, 1)
                act.wait_ge(s_act, chain[0])

            def rsqrt_seed(k, g, var_ap, wait, value, done):
                act.wait_ge(wait, value)
                link(act.activation(lnr[k][g % 2][:, :], var_ap, ACT.Ln, bias=eps_c[:, 0:1]))
                act.activation(r0[k][g % 2][:, :], lnr[k][g % 2][:, :], ACT.Exp, scale=-0.5).then_inc(done, 1)

            for l in range(2):
                act.wait_ge(s_wt, l + 1)
                for m in range(3):
                    ins = act.copy(WT[l][m][:, :], bank[l][:, m * D:(m + 1) * D])
                ins.then_inc(s_wtc, 1)
            act.wait_ge(s_small, 16 * 13)
            act.activation(tanh_g[:, :], graw[:, :], ACT.Tanh).then_inc(s_tanh, 1)
            act.wait_ge(s_gate, 1)
            link(act.activation(wg_ln[:, :], wg_ss[:, :], ACT.Ln))
            act.activation(wg_r[:, :], wg_ln[:, :], ACT.Exp, scale=-0.5).then_inc(s_gate, 1)

            def attention(l):
                def step(i):
                    a, b, c = i - 1, i + 1, i + 2
                    if 0 <= b < G and l == 0:
                        act.wait_ge(s_cT, b + 1)
                        act.copy(ctxT[:, cols(b)], pC[:, :]).then_inc(s_cTc, 1)
                    if 0 <= b < G:
                        act.wait_ge(s_xT, n(l, b))
                        if n(l, b) > 2:
                            act.wait_ge(s_q, n(l, b) - 2)
                        act.copy(xnT[b % 2][:, :], pT[:, :]).then_inc(s_xTc, 1)
                    if 0 <= i < G:
                        act.wait_ge(s_sub, n(l, i))
                        if n(l, i) > 2:
                            act.wait_ge(s_prn, n(l, i) - 2)
                        act.activation(pr[i % 2][:, :, :], sc[i % 2][:, :, :], ACT.Exp,
                                       scale=D ** -0.5 if l == 0 else 1.0).then_inc(s_exp, 1)
                    if 0 <= c < G:
                        rsqrt_seed("A", c, mvA[c % 2][:, :, 1], s_stA, n(l, c), s_r0A)
                    if 0 <= a < G and l == 0:
                        rsqrt_seed("C", a, vC[a % 2][:, :], s_vC, a + 1, s_r0C)
                    if 0 <= b < G:
                        act.wait_ge(s_k, n(l, b))
                        act.activation(kT[b % 2][:, :], pK[:, :], ACT.Identity,
                                       bias=bias_qk[:, 2 * l + 1:2 * l + 2]).then_inc(s_kc, 1)
                    if 0 <= a < G:
                        act.wait_ge(s_x2T, n(l, a))
                        if n(l, a) > 2:
                            act.wait_ge(s_lg, n(l, a) - 2)
                        act.copy(xn2T[a % 2][:, :], pT[:, :]).then_inc(s_x2Tc, 1)
                    if 0 <= i < G:
                        act.wait_ge(s_pT, n(l, i))
                        if n(l, i) > 2:
                            act.wait_ge(s_pv, n(l, i) - 2)
                        pP3 = pP[0:S, :].rearrange("p (j c) -> p j c", j=GT)
                        for h in range(2):
                            part = slice(h * S, (h + 1) * S)
                            ins = act.copy(prT[i % 2][part, :, part], pP3[:, :, part])
                        ins.then_inc(s_pTc, 1)
                    if 0 <= b < G:
                        act.wait_ge(s_q, n(l, b))
                        act.activation(qT[b % 2][:, :], pQ[:, :], ACT.Identity,
                                       bias=bias_qk[:, 2 * l:2 * l + 1]).then_inc(s_qc, 1)
                    if 0 <= i < G:
                        rsqrt_seed("B", i, mvB[i % 2][:, :, 1], s_stB, n(l, i), s_r0B)
                    if 0 <= a < G and l == 1:
                        act.wait_ge(s_gsub, a + 1)
                        act.activation(gs[:, :, :], gl[:, :, :], ACT.Exp).then_inc(s_gexp, 1)
                each_step(l, step)

            def mlp(l):
                func = ACT.Relu if l == 0 else ACT.Gelu

                def step(q, r):
                    q2, r2 = ahead(q, r, 2)
                    if l == 1 and valid(q2, r2):
                        act.wait_ge(s_rt, ST + num(q2, r2) + 1)
                        act.wait_ge(s_h, ST + num(q2, r2) - 2)
                        act.copy(rT[r2 % 3][:, :], pX[:, 0:P]).then_inc(s_rtc, 1)
                    if valid(q, r):
                        act.wait_ge(s_ht, l * ST + num(q, r) + 1)
                        if has_before(l, q, r, 3):
                            act.wait_ge(s_y, l * ST + num(q, r) - 2)
                        act.activation(hT[r % 3][:, :], pHT[r % 3][:, :], func).then_inc(s_hTc, 1)
                each_tile(act, 2, 0, step)

            attention(0)
            for k in range(2 * E):
                act.wait_ge(s_wt, 2 + k + 1)
                to = W1[0] if k < E else W2[0]
                act.copy(to[:, (k % E) * F:(k % E + 1) * F], bank[1 + k % 2][:, :]).then_inc(s_wtc, 1)
            act.wait_ge(s_azs, 1)
            act.activation(alpha[:, :], top[:, :], ACT.Exp, scale=-1.0).then_inc(s_aexp, 1)
            mlp(0)
            attention(1)
            mlp(1)

        @block.vector
        def _(dve):
            chain = [0]

            def link(ins):
                chain[0] += 1
                ins.then_inc(s_dve, 1)
                dve.wait_ge(s_dve, chain[0])

            link(dve.memset(eps_c[:, :], EPS))
            dve.wait_ge(s_small, 16 * 13)
            link(dve.tensor_tensor(wg_sq[:, :], wg_raw[:, :], wg_raw[:, :], ALU.mult))
            link(dve.reduce_sum(wg_ss[:, :], wg_sq[:, :], X_AXIS))
            dve.tensor_scalar(wg_ss[:, :], wg_ss[:, :], GATE_EPS ** 2, None, ALU.max).then_inc(s_gate, 1)
            dve.wait_ge(s_gate, 2)
            link(dve.tensor_tensor(wg_t[:, 0:1], wg_r[:, :], wg_r[:, :], ALU.mult))
            link(dve.tensor_tensor(wg_t[:, 1:2], wg_t[:, 0:1], wg_ss[:, :], ALU.mult))
            link(dve.tensor_scalar(wg_t[:, 2:3], wg_t[:, 1:2], -0.5, 1.5, ALU.mult, ALU.add))
            link(dve.tensor_tensor(wg_t[:, 0:1], wg_t[:, 2:3], wg_r[:, :], ALU.mult))
            dve.tensor_scalar(wg_u[:, :], wg_raw[:, :], wg_t[:, 0:1], None, ALU.mult).then_inc(s_gate, 1)
            dve.wait_ge(s_gate, 4)
            dve.tensor_copy(gateT[0][:, :], bank[2][:, 0:E])
            dve.tensor_copy(ln_gT[:, :], bank[2][:, E:2 * E])
            dve.tensor_copy(ln_bT[:, :], bank[2][:, 2 * E:3 * E])
            dve.tensor_copy(wg_uT[:, :], bank[2][0:R, 3 * E:4 * E]).then_inc(s_gate, 1)
            dve.wait_ge(s_gate, 6)
            link(dve.tensor_copy(gateT[1][:, :], bank[3][:, 0:E]))
            dve.wait_ge(s_tanh, 1)
            dve.wait_ge(s_const, N_CONST)

            def stats(g, mv, done):
                for j in range(GT):
                    ins = dve.bn_stats(bn6[:, j, :], X[:, g * W + j * D:g * W + (j + 1) * D])
                link(ins)
                for j in range(GT):
                    ins = dve.bn_aggr(mv[g % 2][:, j, :], bn6[:, j, :])
                ins.then_inc(done, 1)

            def refine(r, seed, var, done):
                link(dve.tensor_tensor(nt[:, 0, :], seed, seed, ALU.mult))
                link(dve.scalar_tensor_tensor(nt[:, 1, :], var, eps_c[:, 0:1], nt[:, 0, :], ALU.add, ALU.mult))
                link(dve.tensor_scalar(nt[:, 2, :], nt[:, 1, :], -0.5, 1.5, ALU.mult, ALU.add))
                dve.tensor_tensor(r, nt[:, 2, :], seed, ALU.mult).then_inc(done, 1)

            def attention(l):
                def step(i):
                    a, b, c = i - 1, i + 1, i + 2
                    if 0 <= a < G:
                        if n(l, a) > 2:
                            dve.wait_ge(s_rowp, n(l, a) - 2)
                        dve.wait_ge(s_r0B, n(l, a))
                        refine(rs["B"][a % 2][:, :], r0["B"][a % 2][:, :], mvB[a % 2][:, :, 1], s_rsB)
                        if l == 0:
                            dve.wait_ge(s_rsB, a + 1)
                            link(dve.tensor_tensor(nt[:, 0, :], rs["B"][a % 2][:, :], rs["B"][a % 2][:, :], ALU.mult))
                            dve.tensor_tensor(vC[a % 2][:, :], mvB[a % 2][:, :, 1], nt[:, 0, :], ALU.mult
                                              ).then_inc(s_vC, 1)
                    if 0 <= i < G:
                        dve.wait_ge(s_sc, n(l, i))
                        ps = pS[:, 0:GT * S].rearrange("p (j c) -> p j c", j=GT)
                        link(dve.reduce_max(mx[:, :], ps, X_AXIS))
                        dve.tensor_tensor(sc[i % 2][:, :, :], ps, mx[:, :].unsqueeze(2).to_broadcast([P, GT, S]),
                                          ALU.subtract).then_inc(s_sub, 1)
                    if 0 <= c < G:
                        if l == 0:
                            dve.wait_ge(s_in[c % 2], 32 * (c // 2 + 1))
                        else:
                            dve.wait_ge(s_yback[c % 2], 16 * GT * (c // 2 + 1))
                            for j in range(GT):
                                xs = X[:, c * W + j * D:c * W + (j + 1) * D]
                                ins = dve.scalar_tensor_tensor(xs, ymlp[c % 2][:, j * D:(j + 1) * D],
                                                               alpha[:, c * GT + j:c * GT + j + 1], xs,
                                                               ALU.mult, ALU.add)
                            link(ins)
                        if n(l, c) > 2:
                            dve.wait_ge(s_xn, n(l, c) - 2)
                        stats(c, mvA, s_stA)
                    if 0 <= b < G:
                        dve.wait_ge(s_v, n(l, b))
                        dve.tensor_tensor(v[b % 2][:, :, :], tiles3(pV[:, :]),
                                          bias_v[:, l:l + 1, :].to_broadcast([P, GT, D]), ALU.add
                                          ).then_inc(s_vc, 1)
                    if 0 <= i < G:
                        dve.wait_ge(s_exp, n(l, i))
                        link(dve.reduce_sum(den[:, :], pr[i % 2][:, :, :], X_AXIS))
                        link(dve.reciprocal(rden[:, :], den[:, :]))
                        dve.tensor_scalar(rdg[i % 2][:, :], rden[:, :], tanh_g[:, l:l + 1], None, ALU.mult
                                          ).then_inc(s_rd, 1)
                    if 0 <= a < G and l == 0:
                        dve.wait_ge(s_r0C, a + 1)
                        refine(rs["C"][a % 2][:, :], r0["C"][a % 2][:, :], vC[a % 2][:, :], s_rsC)
                    if 0 <= c < G:
                        dve.wait_ge(s_r0A, n(l, c))
                        refine(rs["A"][c % 2][:, :], r0["A"][c % 2][:, :], mvA[c % 2][:, :, 1], s_rsA)
                    if 0 <= a < G:
                        dve.wait_ge(s_xn2, n(l, a))
                        if l == 0:
                            dve.scalar_tensor_tensor(tiles3(X[:, cols(a)]), xn2[a % 2][:, :, :], tanh_g[:, 2:3],
                                                     tiles3(X[:, cols(a)]), ALU.mult, ALU.add).then_inc(s_x2, 1)
                        dve.wait_ge(s_lg, n(l, a))
                        lg = LG[:, a * GT:(a + 1) * GT, :]
                        dve.tensor_copy(lg, pL.rearrange("p (j e) -> p j e", j=GT)).then_inc(s_lgc, 1)
                        if l == 1:
                            dve.wait_ge(s_lgc, n(l, a))
                            link(dve.reduce_max(gm[:, :], lg, X_AXIS))
                            dve.tensor_tensor(gl[:, :, :], lg, gm[:, :].unsqueeze(2).to_broadcast([P, GT, E]),
                                              ALU.subtract).then_inc(s_gsub, 1)
                    if 0 <= i < G:
                        dve.wait_ge(s_pv, n(l, i))
                        dve.tensor_tensor(X[:, cols(i)], X[:, cols(i)], pO[:, :], ALU.add).then_inc(s_x1, 1)
                        dve.wait_ge(s_x1, n(l, i))
                        if n(l, i) > 2:
                            dve.wait_ge(s_rowp, n(l, i) - 2)
                        stats(i, mvB, s_stB)
                    if 0 <= a < G:
                        if l == 1:
                            dve.wait_ge(s_gexp, a + 1)
                            link(dve.reduce_sum(gd[:, :], gs[:, :, :], X_AXIS))
                            link(dve.reciprocal(gm[:, :], gd[:, :]))
                            dve.wait_ge(s_rowp, n(l, a))
                            dve.tensor_scalar(hat[a % 2][:, :, 2 * D], gm[:, :], tanh_g[:, 3:4], None, ALU.mult
                                              ).then_inc(s_row, 1)
                each_step(l, step)

            def route(l):
                dve.wait_ge(s_lgc, n(l, G - 1))
                ins = dve.reduce_max(top[:, :], LG[:, :, :], X_AXIS)
                if l == 0:
                    ins.then_inc(s_azs, 1)
                    dve.wait_ge(s_azs, 1)
                else:
                    link(ins)
                te = [P, TILES, E]
                link(dve.tensor_tensor(hit[:, :, :], LG[:, :, :], top[:, :].unsqueeze(2).to_broadcast(te), ALU.is_equal))
                link(dve.tensor_tensor(hit[:, :, :], hit[:, :, :], iota_e[:, :].unsqueeze(1).to_broadcast(te), ALU.mult))
                link(dve.tensor_reduce(first[:, :], hit[:, :, :], X_AXIS, ALU.min))
                link(dve.tensor_tensor(oh[:, :, :].rearrange("p e t -> p t e"), first[:, :].unsqueeze(2).to_broadcast(te),
                                       iota_e[:, :].unsqueeze(1).to_broadcast(te), ALU.is_equal))
                dve.reduce_sum(cnt[:, :], oh[:, :, :], X_AXIS).then_inc(s_cnt, 1)
                link(dve.tensor_tensor_scan(cum[:, :, :].rearrange("p e t -> p (e t)"), ones_et[:, :],
                                            oh[:, :, :].rearrange("p e t -> p (e t)"), 0.0, ALU.mult, ALU.add))
                dve.wait_ge(s_pfx, l + 1)
                link(dve.tensor_scalar(tf[:, :], bank[0][:, E:2 * E], float(P - 1), None, ALU.add))
                link(dve.tensor_copy(ti[:, :], tf[:, :]))
                link(dve.tensor_scalar(ti[:, :], ti[:, :], 7, None, ALU.logical_shift_right))
                link(dve.tensor_copy(tcnt[:, :], ti[:, :]))
                link(dve.tensor_tensor_scan(tend[:, :], ones_et[:, 0:E], tcnt[:, :], 0.0, ALU.mult, ALU.add))
                link(dve.tensor_tensor(ends[:, :], tend[:, :], tcnt[:, :], ALU.subtract))
                link(dve.tensor_scalar(ends[:, :], ends[:, :], float(P), -1.0, ALU.mult, ALU.add))
                link(dve.tensor_tensor(off[:, :], ends[:, :], bank[0][:, 0:E], ALU.add))
                link(dve.tensor_tensor(ends[:, :], cum[:, :, TILES - 1], cnt[:, :], ALU.subtract))
                link(dve.tensor_tensor(off[:, :], off[:, :], ends[:, :], ALU.subtract))
                et = [P, E, TILES]
                link(dve.tensor_tensor(cum[:, :, :], cum[:, :, :], off[:, :].unsqueeze(2).to_broadcast(et), ALU.add))
                link(dve.tensor_tensor(cum[:, :, :], cum[:, :, :], oh[:, :, :], ALU.mult))
                link(dve.reduce_sum(slot_f[:, :], cum[:, :, :].rearrange("p e t -> p t e"), X_AXIS))
                link(dve.tensor_copy(slot[:, :], slot_f[:, :]))
                dve.tensor_scalar(hi_i[:, :], slot[:, :], 7, None, ALU.logical_shift_right)
                link(dve.tensor_scalar(lo_i[:, :], slot[:, :], P - 1, None, ALU.bitwise_and))
                dve.tensor_copy(hi[:, :], hi_i[:, :])
                dve.tensor_copy(lo[:, :], lo_i[:, :]).then_inc(s_hilo, 1)
                dve.wait_ge(s_hilo, l + 1)
                for tt in range(TILES):
                    if l * TILES + tt >= 4:
                        dve.wait_ge(s_invm, l * TILES + tt - 3)
                    dve.tensor_scalar(in_lo[tt % 4][:, :], iota_p[:, :], lo[:, tt:tt + 1], None, ALU.is_equal
                                      ).then_inc(s_lo, 1)
                se = [P, ST, E]
                link(dve.tensor_tensor(ge[:, :, :], iota_s[:, :].unsqueeze(2).to_broadcast(se),
                                       tend[:, :].unsqueeze(1).to_broadcast(se), ALU.is_ge))
                link(dve.reduce_sum(eid_f[:, :], ge[:, :, :], X_AXIS))
                link(dve.tensor_scalar(eid_f[:, :], eid_f[:, :], float(E - 1), None, ALU.min))
                dve.tensor_copy(eid[:, :], eid_f[:, :]).then_inc(s_eid, 1)
                dve.wait_ge(s_invm, (l + 1) * TILES)
                link(dve.tensor_copy(inv_f[:, :], bank[3][:, 0:ST]))
                link(dve.tensor_scalar(src_f[:, :], inv_f[:, :], -1.0, 0.0, ALU.add, ALU.max))
                if l == 1:
                    link(dve.tensor_scalar(dst_f[:, :], inv_f[:, :], 0.0, EMPTY, ALU.is_equal, ALU.mult))
                    link(dve.tensor_tensor(dst_f[:, :], dst_f[:, :], src_f[:, :], ALU.add))
                    link(dve.tensor_copy(dst[:, :], dst_f[:, :]))
                dve.tensor_copy(src[:, :], src_f[:, :]).then_inc(s_src, 1)
                if l == 0:
                    dve.wait_ge(s_aexp, 1)
                    link(dve.tensor_scalar(alpha[:, :], alpha[:, :], 1.0, None, ALU.add))
                    link(dve.reciprocal(alpha[:, :], alpha[:, :]))
                    link(dve.tensor_scalar(alpha[:, :], alpha[:, :], tanh_g[:, 2:3], None, ALU.mult))

            def mlp(l):
                base = l * ST
                dve.wait_ge(s_eid, l + 1)
                dve.wait_ge(s_wload[3], 48 + 16 * l)

                def expert(q, r):
                    return dve.value_load(eid[0:1, bass.ds(num(q, r), 1)], min_val=0, max_val=E - 1)

                def step(q, r):
                    q2, r2 = ahead(q, r, 2)
                    q1, r1 = ahead(q, r, 1)
                    q0, rp = ahead(q, r, -1)
                    if l == 0 and valid(q2, r2):
                        ev = expert(q2, r2)
                        dve.wait_ge(s_rt, num(q2, r2) + 1)
                        if has_before(0, q2, r2, 3):
                            dve.wait_ge(s_h, num(q2, r2) - 2)
                        dve.tensor_scalar(rT[r2 % 3][:, :], pX[:, 0:P], ln_gT[:, bass.ds(ev, 1)],
                                          ln_bT[:, bass.ds(ev, 1)], ALU.mult, ALU.add).then_inc(s_rtc, 1)
                    if valid(q1, r1):
                        ev = expert(q1, r1)
                        dve.wait_ge(s_h, base + num(q1, r1) + 1)
                        if has_before(l, q1, r1, 3):
                            dve.wait_ge(s_ht, base + num(q1, r1) - 2)
                        dve.tensor_tensor(hb[r1 % 3][:, :], pH[r1 % 3][:, :], B1[:, bass.ds(ev * F, F)], ALU.add
                                          ).then_inc(s_hb, 1)
                    if valid(q0, rp):
                        ev = expert(q0, rp)
                        dve.wait_ge(s_y, base + num(q0, rp) + 1)
                        if l == 0:
                            if has_before(0, q0, rp, 3):
                                dve.wait_ge(s_out[rp % 3], 16 * third(q0, rp))
                            dve.tensor_tensor(yb[rp % 3][:, :], pY[:, 0:D], B2[l][:, bass.ds(ev * D, D)], ALU.add
                                              ).then_inc(s_yb, 1)
                        else:
                            if has_before(0, q0, rp, 3):
                                dve.wait_ge(s_scat[rp % 3], 16 * third(q0, rp))
                            link_y(dve.tensor_tensor(yb[rp % 3][:, :], pY[:, 0:D], B2[l][:, bass.ds(ev * D, D)], ALU.add),
                                   num(q0, rp) + 1)
                            dve.scalar_tensor_tensor(ob[rp % 3][:, :], yb[rp % 3][:, :], rows[rp][:, 2 * D:2 * D + 1],
                                                     rows[rp][:, D:2 * D], ALU.mult, ALU.add).then_inc(s_yb, 1)

                def link_y(ins, value):
                    ins.then_inc(s_y1, 1)
                    dve.wait_ge(s_y1, value)
                each_tile(dve, 2, 1, step)

            attention(0)
            route(0)
            mlp(0)
            attention(1)
            route(1)
            mlp(1)

        @block.tensor
        def _(pe):
            pe.wait_ge(s_const, N_CONST)
            pe.wait_ge(s_wload[0], 96)
            for l in range(2):
                for m in range(3):
                    ins = pe.transpose(bank[l][:, m * D:(m + 1) * D], WT[l][m][:, :], ident[:, :])
                ins.then_inc(s_wt, 1)
            pe.wait_ge(s_small, 16 * 13)
            pe.wait_ge(s_gate, 3)
            for m in range(3):
                pe.transpose(bank[2][:, m * E:(m + 1) * E], raw_small[:, m, :], ident[0:E, 0:E])
            pe.transpose(bank[2][0:R, 3 * E:4 * E], wg_u[:, :], ident[0:E, 0:E]).then_inc(s_gate, 1)
            pe.wait_ge(s_gate, 5)
            pe.matmul(bank[3][:, 0:E], wg_red[:, :], wg_uT[:, :], start=True, stop=True).then_inc(s_gate, 1)
            pe.wait_ge(s_gate, 6)
            pe.wait_ge(s_wtc, 2)

            def tile_of(ap, j, w=D):
                return ap[:, j * w:(j + 1) * w]

            def attention(l):
                wq, wk, wv = (w[:, :] for w in WT[l])

                def step(i):
                    a, b = i - 1, i + 1
                    if 0 <= b < G and l == 0:
                        pe.wait_ge(s_in[b % 2], 32 * (b // 2 + 1))
                        if b >= 1:
                            pe.wait_ge(s_cTc, b)
                        for j in range(GT):
                            ins = pe.transpose(tile_of(pC, j), ctx_raw[b % 2][:, j, :], ident[:, :])
                        ins.then_inc(s_cT, 1)
                    if 0 <= i < G:
                        pe.wait_ge(s_kc, n(l, i))
                        pe.wait_ge(s_qc, n(l, i))
                        if n(l, i) > 1:
                            pe.wait_ge(s_sub, n(l, i) - 1)
                            if n(l, i) > 2:
                                pe.wait_ge(s_lgc, n(l, i) - 2)
                            pe.wait_ge(s_lgc, l * G) if l == 1 else None
                        for j in range(GT):
                            for h in range(2):
                                c = j * P + h * S
                                ins = pe.matmul(pS[h * S:(h + 1) * S, j * S:(j + 1) * S], qT[i % 2][:, c:c + S],
                                                kT[i % 2][:, c:c + S], start=True, stop=True)
                        ins.then_inc(s_sc, 1)
                    if 0 <= b < G:
                        pe.wait_ge(s_xn, n(l, b))
                        if b >= 3:
                            pe.wait_ge(s_x2Tc, n(l, b - 3))
                        if n(l, b) > 1:
                            pe.wait_ge(s_xTc, n(l, b) - 1)
                        for j in range(GT):
                            ins = pe.transpose(tile_of(pT, j), xn[b % 2][:, j, :], ident[:, :])
                        ins.then_inc(s_xT, 1)
                        cT = ctxT[:, cols(b)]
                        if l == 0:
                            pe.wait_ge(s_cTc, b + 1)
                        if n(l, b) > 1:
                            pe.wait_ge(s_kc, n(l, b) - 1)
                            pe.wait_ge(s_vc, n(l, b) - 1)
                        pe.matmul(pK[:, :], wk, cT, start=True, stop=True).then_inc(s_k, 1)
                        for j in range(GT):
                            ins = pe.matmul(tile_of(pV, j), tile_of(cT, j), wv, start=True, stop=True)
                        ins.then_inc(s_v, 1)
                    if 0 <= i < G:
                        pe.wait_ge(s_prn, n(l, i))
                        if n(l, i) > 1:
                            pe.wait_ge(s_pTc, n(l, i) - 1)
                        for j in range(GT):
                            ins = pe.transpose(pP[0:S, j * P:(j + 1) * P], prn[i % 2][:, j, :], ident[:, :])
                        ins.then_inc(s_pT, 1)
                    if 0 <= b < G:
                        pe.wait_ge(s_xTc, n(l, b))
                        if n(l, b) > 1:
                            pe.wait_ge(s_qc, n(l, b) - 1)
                        pe.matmul(pQ[:, :], wq, xnT[b % 2][:, :], start=True, stop=True).then_inc(s_q, 1)
                    if 0 <= a < G:
                        pe.wait_ge(s_xn2, n(l, a))
                        pe.wait_ge(s_xTc, n(l, min(b, G - 1)))
                        for j in range(GT):
                            ins = pe.transpose(tile_of(pT, j), xn2[a % 2][:, j, :], ident[:, :])
                        ins.then_inc(s_x2T, 1)
                    if 0 <= i < G:
                        pe.wait_ge(s_pTc, n(l, i))
                        pe.wait_ge(s_vc, n(l, i))
                        if n(l, i) > 1:
                            pe.wait_ge(s_x1, n(l, i) - 1)
                        for j in range(GT):
                            ins = pe.matmul(tile_of(pO, j), prT[i % 2][:, j, :], v[i % 2][:, j, :],
                                            start=True, stop=True)
                        ins.then_inc(s_pv, 1)
                    if 0 <= a < G:
                        pe.wait_ge(s_x2Tc, n(l, a))
                        if n(l, a) > 1:
                            pe.wait_ge(s_lgc, n(l, a) - 1)
                        if i < G:
                            pe.wait_ge(s_sub, n(l, i))
                        for j in range(GT):
                            ins = pe.matmul(tile_of(pL, j, E), tile_of(xn2T[a % 2], j), gateT[l][:, :],
                                            start=True, stop=True)
                        ins.then_inc(s_lg, 1)
                each_step(l, step)

            def route(l):
                pe.wait_ge(s_cnt, l + 1)
                pe.matmul(bank[0][:, 0:E], before[:, :], cnt[:, :], start=True, stop=True)
                pe.matmul(bank[0][:, E:2 * E], ones[:, :], cnt[:, :], start=True, stop=True).then_inc(s_pfx, 1)
                if l == 0:
                    pe.wait_ge(s_wload[1], 16)
                    pe.wait_ge(s_wload[2], 16)
                    for k in range(2 * E):
                        if k >= 2:
                            pe.wait_ge(s_wtc, 2 + k - 1)
                        raw = W1[1] if k < E else W2[1]
                        for c in range(FC):
                            col = (k % E) * F + c * P
                            ins = pe.transpose(bank[1 + k % 2][:, c * P:(c + 1) * P], raw[:, col:col + P], ident[:, :])
                        ins.then_inc(s_wt, 1)
                for tt in range(TILES):
                    pe.wait_ge(s_lo, l * TILES + tt + 1)
                    pe.wait_ge(s_hi, l * TILES + tt + 1)
                    pe.matmul(bank[3][:, 0:ST], in_lo[tt % 4][:, :], in_hi[tt % 4][:, :],
                              start=(tt == 0), stop=(tt == TILES - 1)).then_inc(s_invm, 1)
                if l == 0:
                    pe.wait_ge(s_wtc, 2 + 2 * E)
                else:
                    pe.wait_ge(s_l1w, 32)

            def mlp(l):
                base = l * ST
                pe.wait_ge(s_eid, l + 1)
                pe.wait_ge(s_src, l + 1)

                def expert(q, r):
                    return pe.value_load(eid[0:1, bass.ds(num(q, r), 1)], min_val=0, max_val=E - 1)

                def step(q, r):
                    q2, r2 = ahead(q, r, 2)
                    q1, r1 = ahead(q, r, 1)
                    q0, rp = ahead(q, r, -1)
                    if valid(q2, r2):
                        pe.wait_ge(s_row_in[l][r2], 16 * (q2 + 1))
                        if has_before(l, q2, r2, 1):
                            pe.wait_ge(s_rtc, base + num(q2, r2))
                        pe.transpose(pX[:, 0:P], rows[r2][:, 0:D], ident[:, :]).then_inc(s_rt, 1)
                    if valid(q1, r1):
                        ev = expert(q1, r1)
                        pe.wait_ge(s_rtc, base + num(q1, r1) + 1)
                        if has_before(l, q1, r1, 3):
                            pe.wait_ge(s_hb, base + num(q1, r1) - 2)
                        pe.matmul(pH[r1 % 3][:, :], rT[r1 % 3][:, :], W1[l][:, bass.ds(ev * F, F)],
                                  start=True, stop=True).then_inc(s_h, 1)
                    if valid(q, r):
                        pe.wait_ge(s_hb, base + num(q, r) + 1)
                        if has_before(l, q, r, 3):
                            pe.wait_ge(s_hTc, base + num(q, r) - 2)
                        for c in range(FC):
                            ins = pe.transpose(pHT[r % 3][:, c * P:(c + 1) * P], hb[r % 3][:, c * P:(c + 1) * P], ident[:, :])
                        ins.then_inc(s_ht, 1)
                    if valid(q0, rp):
                        ev = expert(q0, rp)
                        pe.wait_ge(s_hTc, base + num(q0, rp) + 1)
                        if has_before(l, q0, rp, 1):
                            pe.wait_ge(s_yb, base + num(q0, rp))
                        for c in range(FC):
                            ins = pe.matmul(pY[:, 0:D], hT[rp % 3][:, c * P:(c + 1) * P],
                                            W2[l][:, bass.ds(ev * F + c * P, P)],
                                            start=(c == 0), stop=(c == FC - 1))
                        ins.then_inc(s_y, 1)
                each_tile(pe, 2, 1, step)

            attention(0)
            route(0)
            mlp(0)
            attention(1)
            route(1)
            mlp(1)


_INS = ["x", "ctx_1024", "g_xattn", "g_ffn",
        "L0_xattn_Wq", "L0_xattn_bq", "L0_xattn_Wk", "L0_xattn_bk", "L0_xattn_Wv", "L0_xattn_bv",
        "L0_ffn_centroids", "L0_ffn_ln_g", "L0_ffn_ln_b", "L0_ffn_w1", "L0_ffn_b1", "L0_ffn_w2", "L0_ffn_b2",
        "L1_xattn_Wq", "L1_xattn_bq", "L1_xattn_Wk", "L1_xattn_bk", "L1_xattn_Wv", "L1_xattn_bv",
        "L1_ffn_wg_red", "L1_ffn_wg", "L1_ffn_w1", "L1_ffn_b1", "L1_ffn_w2", "L1_ffn_b2"]


def kernel(**inputs):
    import numpy as _np
    import concourse.bacc as _bacc
    from concourse import mybir as _mybir
    from concourse.bass_utils import run_bass_kernel_spmd as _run

    nc = _bacc.Bacc("TRN2", target_bir_lowering=False, num_devices=1)
    arrays, args = {}, {}
    for name in _INS:
        a = _np.ascontiguousarray(inputs[name])
        arrays[f"in_{name}_dram"] = a
        args[name] = nc.dram_tensor(f"in_{name}_dram", a.shape, _mybir.dt.from_np(a.dtype), kind="ExternalInput").ap()
    out = nc.dram_tensor("out_0_dram", tuple(inputs["x"].shape), _mybir.dt.float32, kind="ExternalOutput").ap()
    build(nc, args, out)
    r = _run(nc, [arrays], core_ids=[0])
    return r.results[0]["out_0_dram"]
```

```python
from contextlib import ExitStack

import concourse.bass as bass
from concourse import mybir

F32 = mybir.dt.float32
I32 = mybir.dt.int32
ALU = mybir.AluOpType
ACT = mybir.ActivationFunctionType
X_AXIS = mybir.AxisListType.X

P = 128
EPS = 1e-5
GATE_EPS = 1e-4
EMPTY = 8192.0


def build(nc, t, out):
    B, S, D = t["x"].shape
    E, F, _ = t["L0_ffn_w1"].shape
    R = t["L1_ffn_wg_red"].shape[0]
    TOK = B * S
    TILES = TOK // P
    GT = 4
    G = TILES // GT
    W = GT * D
    FC = F // P
    ST = TILES + E - 1
    RW = 2 * D + 4
    assert D == P and S * 2 == P and ST % 3 == 0 and P // 2 == S

    x_rows = t["x"].rearrange("b s d -> (b s) d")
    ctx_rows = t["ctx_1024"].rearrange("b s d -> (b s) d")
    out_rows = out.rearrange("b s d -> (b s) d")
    tok_rows = [nc.dram_tensor("tok_rows0", [TOK, D], F32, kind="Internal").ap(),
                nc.dram_tensor("tok_rows1", [TOK, RW], F32, kind="Internal").ap()]
    mlp_rows = nc.dram_tensor("mlp_rows", [ST * P, D], F32, kind="Internal").ap()

    with ExitStack() as ctx:
        def sb(name, shape, dt=F32):
            return ctx.enter_context(nc.sbuf_tensor(name, shape, dt))

        def sem(name):
            return ctx.enter_context(nc.semaphore(name))

        X = sb("X", [P, TOK])
        ctxT = sb("ctxT", [P, TOK])
        WT = [[sb(f"WT{l}{m}", [P, D]) for m in "qkv"] for l in range(2)]
        bias_qk = sb("bias_qk", [P, 4])
        bias_v = sb("bias_v", [P, 2, D])
        W1 = [sb(f"W1_{l}", [P, E * F]) for l in range(2)]
        W2 = [sb(f"W2_{l}", [P, E * F]) for l in range(2)]
        B1 = sb("B1", [P, E * F])
        B2 = [sb(f"B2_{l}", [P, E * D]) for l in range(2)]
        ln_gT, ln_bT = sb("ln_gT", [P, E]), sb("ln_bT", [P, E])
        gateT = [sb("gateT0", [P, E]), sb("gateT1", [P, E])]
        tanh_g = sb("tanh_g", [P, 4])
        ident, ones = sb("ident", [P, P]), sb("ones", [P, P])
        before = sb("before", [P, P])
        iota_e = sb("iota_e", [P, E])
        iota_p = sb("iota_p", [P, P])
        iota_s = sb("iota_s", [P, ST])
        token1 = sb("token1", [P, TILES])

        raw_small = sb("raw_small", [E, 3, D])
        wg_raw, wg_red = sb("wg_raw", [E, R]), sb("wg_red", [R, D])
        wg_sq, wg_ss, wg_ln = sb("wg_sq", [E, R]), sb("wg_ss", [E, 1]), sb("wg_ln", [E, 1])
        wg_r, wg_t, wg_u = sb("wg_r", [E, 1]), sb("wg_t", [E, 3]), sb("wg_u", [E, R])
        wg_uT = sb("wg_uT", [R, E])
        graw = sb("graw", [P, 4])

        ctx_raw = [sb(f"ctx_raw{i}", [P, GT, D]) for i in range(2)]
        xn = [sb(f"xn{i}", [P, GT, D]) for i in range(2)]
        xnT = [sb(f"xnT{i}", [P, W]) for i in range(2)]
        qT = [sb(f"qT{i}", [P, W]) for i in range(2)]
        kT = [sb(f"kT{i}", [P, W]) for i in range(2)]
        v = [sb(f"v{i}", [P, GT, D]) for i in range(2)]
        sc = [sb(f"sc{i}", [P, GT, S]) for i in range(2)]
        pr = [sb(f"pr{i}", [P, GT, S]) for i in range(2)]
        prn = [sb(f"prn{i}", [P, GT, S]) for i in range(2)]
        prT = [sb(f"prT{i}", [P, GT, P]) for i in range(2)]
        xn2 = [sb(f"xn2{i}", [P, GT, D]) for i in range(2)]
        xn2T = [sb(f"xn2T{i}", [P, W]) for i in range(2)]
        hat = [sb(f"hat{i}", [P, GT, RW]) for i in range(2)]
        bn6 = sb("bn6", [P, GT, 6])
        mvA = [sb(f"mvA{i}", [P, GT, 2]) for i in range(2)]
        mvB = [sb(f"mvB{i}", [P, GT, 2]) for i in range(2)]
        pin = [sb(f"pin{i}", [P, 3 * GT]) for i in range(2)]
        pout = [sb(f"pout{i}", [P, 3 * GT]) for i in range(2)]
        minus_half = sb("minus_half", [P, 3 * GT])
        mx, den, rden = sb("mx", [P, GT]), sb("den", [P, GT]), sb("rden", [P, GT])
        rdg = [sb(f"rdg{i}", [P, GT]) for i in range(2)]
        ymlp = [sb(f"ymlp{i}", [P, W]) for i in range(2)]

        LG = sb("LG", [P, TILES, E])
        top = sb("top", [P, TILES])
        alpha = sb("alpha", [P, TILES])
        gl, gs = sb("gl", [P, GT, E]), sb("gs", [P, GT, E])
        gm, gd = sb("gm", [P, GT]), sb("gd", [P, GT])
        hit = sb("hit", [P, TILES, E])
        first = sb("first", [P, TILES])
        oh = sb("oh", [P, E, TILES])
        cum = sb("cum", [P, E, TILES])
        ones_et = sb("ones_et", [P, E * TILES])
        cnt, ends = sb("cnt", [P, E]), sb("ends", [P, E])
        tf, ti = sb("tf", [P, E]), sb("ti", [P, E], I32)
        tcnt, tend, off = sb("tcnt", [P, E]), sb("tend", [P, E]), sb("off", [P, E])
        slot_f = sb("slot_f", [P, TILES])
        slot = sb("slot", [P, TILES], I32)
        hi_i, lo_i = sb("hi_i", [P, TILES], I32), sb("lo_i", [P, TILES], I32)
        hi, lo = sb("hi", [P, TILES]), sb("lo", [P, TILES])
        in_lo = [sb(f"in_lo{i}", [P, P]) for i in range(4)]
        in_hi = [sb(f"in_hi{i}", [P, ST]) for i in range(4)]
        ge = sb("ge", [P, ST, E])
        eid_f, eid = sb("eid_f", [P, ST]), sb("eid", [P, ST], I32)
        inv_f, src_f, dst_f = sb("inv_f", [P, ST]), sb("src_f", [P, ST]), sb("dst_f", [P, ST])
        src, dst = sb("src", [P, ST], I32), sb("dst", [P, ST], I32)

        rows = [b[:, :, :].rearrange("p j d -> p (j d)") for b in (*v, *xn, *xn2)]
        rT = [sb(f"rT{i}", [P, P]) for i in range(3)]
        hb = [qT[0], qT[1], kT[0]]
        hT = [kT[1], xnT[0], xnT[1]]
        yb = [sb(f"yb{i}", [P, D]) for i in range(3)]
        ob = [sb(f"ob{i}", [P, D]) for i in range(3)]

        bank = [ctx.enter_context(nc.psum_tensor(f"bank{i}", [P, 512], F32)) for i in range(8)]
        pC, pS, pT, pK, pV, pP, pQ, pO = bank
        pL = pS[:, GT * S:GT * S + GT * E]
        pX, pH, pHT, pY = bank[0], bank[1:4], bank[4:7], bank[7]

        s_const = sem("s_const")
        s_wload = [sem(f"s_wload{i}") for i in range(5)]
        s_small = sem("s_small")
        s_l1w = sem("s_l1w")
        s_wt = sem("s_wt")
        s_wtc = sem("s_wtc")
        s_gate = sem("s_gate")
        s_tanh = sem("s_tanh")
        s_in = [sem(f"s_in{i}") for i in range(2)]
        s_cT, s_cTc = sem("s_cT"), sem("s_cTc")
        s_stA, s_pin, s_pow = sem("s_stA"), sem("s_pin"), sem("s_pow")
        s_xn, s_xT, s_xTc = sem("s_xn"), sem("s_xT"), sem("s_xTc")
        s_q, s_qc, s_k, s_kc, s_v, s_vc = (sem(n) for n in ("s_q", "s_qc", "s_k", "s_kc", "s_v", "s_vc"))
        s_sc, s_sub, s_exp, s_rd, s_prn = (sem(n) for n in ("s_sc", "s_sub", "s_exp", "s_rd", "s_prn"))
        s_pT, s_pTc, s_pv, s_x1 = (sem(n) for n in ("s_pT", "s_pTc", "s_pv", "s_x1"))
        s_xn2, s_x2T, s_x2Tc, s_lg, s_lgc = (sem(n) for n in ("s_xn2", "s_x2T", "s_x2Tc", "s_lg", "s_lgc"))
        s_gsub, s_gexp, s_row, s_rowx = sem("s_gsub"), sem("s_gexp"), sem("s_row"), sem("s_rowx")
        s_powu = sem("s_powu")
        s_store = [sem(f"s_store{i}") for i in range(2)]
        s_yback = [sem(f"s_yback{i}") for i in range(2)]
        s_x2 = sem("s_x2")
        s_dve = sem("s_dve")
        s_act = sem("s_act")
        s_cnt, s_pfx, s_hilo, s_lo, s_invm, s_src, s_eid = (
            sem(n) for n in ("s_cnt", "s_pfx", "s_hilo", "s_lo", "s_invm", "s_src", "s_eid"))
        s_aexp, s_azs = sem("s_aexp"), sem("s_azs")
        s_row_in = [[sem(f"s_row_in{l}{i}") for i in range(6)] for l in range(2)]
        s_rt, s_rtc, s_h, s_hb, s_ht, s_hTc, s_y, s_yb = (
            sem(n) for n in ("s_rt", "s_rtc", "s_h", "s_hb", "s_ht", "s_hTc", "s_y", "s_yb"))
        s_out = [sem(f"s_out{i}") for i in range(3)]
        s_scat = [sem(f"s_scat{i}") for i in range(3)]
        s_y1 = sem("s_y1")
        N_CONST = 12
        STEPS = G + 3

        block = ctx.enter_context(nc.Block())

        def n(l, g):
            return l * G + g + 1

        def cols(g):
            return slice(g * W, (g + 1) * W)

        def tiles3(ap):
            return ap.rearrange("p (j d) -> p j d", j=GT)

        def each_step(l, step):
            for i in range(-2, G + 1):
                step(i)

        U = 6

        def each_tile(eng, lead, tail, step):
            for s in range(-lead, U):
                step(s // U, s % U)
            with eng.Fori(1, ST // U) as q:
                for r in range(U):
                    step(q, r)
            for s in range(ST // U * U, ST + tail):
                step(s // U, s % U)

        def ahead(q, r, k):
            return q + (r + k) // U, (r + k) % U

        def num(q, r):
            return U * q + r

        def third(q, r):
            return U // 3 * q + r // 3

        def valid(q, r):
            return not isinstance(q, int) or 0 <= num(q, r) < ST

        def has_before(l, q, r, k):
            return l == 1 or not isinstance(q, int) or num(q, r) >= k

        @block.sync
        def _(sp):
            def load_group(g):
                for dst_ap, rows_ap in ((tiles3(X[:, cols(g)]), x_rows), (ctx_raw[g % 2][:, :, :], ctx_rows)):
                    sp.dma_start(dst_ap, rows_ap[g * GT * P:(g + 1) * GT * P, :].rearrange("(j p) d -> p j d", p=P)
                                 ).then_inc(s_in[g % 2], 16)

            load_group(0)
            sp.dma_start(graw[:, 0:2], t["g_xattn"].partition_broadcast(P)).then_inc(s_small, 16)
            sp.dma_start(graw[:, 2:4], t["g_ffn"].partition_broadcast(P)).then_inc(s_small, 16)
            for l in range(2):
                for m in range(2):
                    sp.dma_start(bias_qk[:, 2 * l + m:2 * l + m + 1],
                                 t[f"L{l}_xattn_b{'qk'[m]}"].rearrange("(p o) -> p o", o=1)).then_inc(s_small, 16)
                sp.dma_start(bias_v[:, l, :], t[f"L{l}_xattn_bv"].partition_broadcast(P)).then_inc(s_small, 16)
            for m, name in enumerate(("centroids", "ln_g", "ln_b")):
                sp.dma_start(raw_small[:, m, :], t[f"L0_ffn_{name}"]).then_inc(s_small, 16)
            sp.dma_start(wg_raw[:, :], t["L1_ffn_wg"]).then_inc(s_small, 16)
            sp.dma_start(wg_red[:, :], t["L1_ffn_wg_red"]).then_inc(s_small, 16)
            load_group(1)
            sp.dma_start(W1[1][:, :].rearrange("p (e c d) -> p e c d", e=E, c=FC),
                         t["L0_ffn_w1"].rearrange("e (c p) d -> p e c d", p=P)).then_inc(s_wload[1], 16)
            sp.dma_start(W2[1][:, :].rearrange("p (e f) -> p e f", e=E),
                         t["L0_ffn_w2"].rearrange("e p f -> p e f")).then_inc(s_wload[2], 16)
            sp.dma_start(B1[:, :], t["L0_ffn_b1"].rearrange("e f -> (e f)").partition_broadcast(P)
                         ).then_inc(s_wload[3], 16)
            for l in range(2):
                sp.dma_start(B2[l][:, :], t[f"L{l}_ffn_b2"].rearrange("e d -> (e d)").partition_broadcast(P)
                             ).then_inc(s_wload[3], 16)

            def store_rows(l, g):
                sp.wait_ge(s_row, n(l, g))
                if l == 1:
                    sp.wait_ge(s_rowx, g + 1)
                wide = (D, RW)[l]
                sp.dma_start(tok_rows[l][g * GT * P:(g + 1) * GT * P, :].rearrange("(j p) d -> p j d", p=P),
                             hat[g % 2][:, :, 0:wide]).then_inc(s_store[g % 2], 16)

            for g in range(2, G + 4):
                if g < G:
                    sp.wait_ge(s_cT, g - 1)
                    load_group(g)
                if g >= 4:
                    store_rows(0, g - 4)
            sp.wait_ge(s_wt, 2 + 2 * E)
            sp.dma_start(W1[1][:, :].rearrange("p (e f) -> p e f", e=E),
                         t["L1_ffn_w1"].rearrange("e d f -> d e f")).then_inc(s_l1w, 16)
            sp.dma_start(W2[1][:, :].rearrange("p (e c d) -> p e c d", e=E, c=FC),
                         t["L1_ffn_w2"].rearrange("e (c p) d -> p e c d", p=P)).then_inc(s_l1w, 16)

            def store_mlp(q, r):
                q, r = ahead(q, r, -1)
                if not valid(q, r):
                    return
                sp.wait_ge(s_yb, num(q, r) + 1)
                sp.dma_start(mlp_rows[bass.ds((num(q, r)) * P, P), :], yb[r % 3][:, :]).then_inc(s_out[r % 3], 16)

            each_tile(sp, 0, 1, store_mlp)
            sp.wait_ge(s_hb, ST)
            sp.dma_start(B1[:, :], t["L1_ffn_b1"].rearrange("e f -> (e f)").partition_broadcast(P)
                         ).then_inc(s_wload[3], 16)
            for g in range(G):
                store_rows(1, g)
            for r in range(3):
                sp.wait_ge(s_scat[r], 16 * (ST // 3))

        @block.gpsimd
        def _(pool):
            pool.memset(ident[:, :], 0.0).then_inc(s_const, 1)
            pool.memset(before[:, :], 1.0).then_inc(s_const, 1)
            pool.memset(ones[:, :], 1.0).then_inc(s_const, 1)
            pool.iota(iota_e[:, :], [[1, E]], base=-E, channel_multiplier=0,
                      allow_small_or_imprecise_dtypes=True).then_inc(s_const, 1)
            pool.iota(iota_p[:, :], [[1, P]], base=0, channel_multiplier=0,
                      allow_small_or_imprecise_dtypes=True).then_inc(s_const, 1)
            pool.iota(iota_s[:, :], [[1, ST]], base=0, channel_multiplier=0,
                      allow_small_or_imprecise_dtypes=True).then_inc(s_const, 1)
            pool.iota(token1[:, :], [[P, TILES]], base=1, channel_multiplier=1,
                      allow_small_or_imprecise_dtypes=True).then_inc(s_const, 1)
            pool.memset(ones_et[:, :], 1.0).then_inc(s_const, 1)
            pool.wait_ge(s_const, 8)
            pool.affine_select(out=ident[:, :], in_=ident[:, :], compare_op=ALU.not_equal, fill=1.0, base=0,
                               pattern=[[-1, P]], channel_multiplier=1).then_inc(s_const, 1)
            pool.affine_select(out=before[:, :], in_=before[:, :], compare_op=ALU.is_gt, fill=0.0, base=0,
                               pattern=[[1, P]], channel_multiplier=-1).then_inc(s_const, 1)
            pool.memset(minus_half[:, :], -0.5).then_inc(s_const, 1)
            pool.memset(prT[0][:, :, :], 0.0)
            pool.memset(hat[0][:, :, :], 0.0)
            pool.memset(hat[1][:, :, :], 0.0)
            pool.memset(prT[1][:, :, :], 0.0).then_inc(s_const, 1)

            def rsqrt(l, i):
                pool.wait_ge(s_pin, l * STEPS + i + 3)
                if l * STEPS + i >= 0:
                    pool.wait_ge(s_powu, l * STEPS + i + 1)
                pool.tensor_tensor(pout[i % 2][:, :], pin[i % 2][:, :], minus_half[:, :], ALU.pow
                                   ).then_inc(s_pow, 1)

            def norm_probs(l, g):
                pool.wait_ge(s_exp, n(l, g))
                pool.wait_ge(s_rd, n(l, g))
                if n(l, g) > 2:
                    pool.wait_ge(s_pT, n(l, g) - 2)
                pool.tensor_tensor(prn[g % 2][:, :, :], pr[g % 2][:, :, :],
                                   rdg[g % 2][:, :].unsqueeze(2).to_broadcast([P, GT, S]), ALU.mult
                                   ).then_inc(s_prn, 1)

            def gather_back(g):
                if g >= 2:
                    pool.wait_ge(s_stA, g - 1)
                for j in range(GT):
                    pool.indirect_dma_start(ymlp[g % 2][:, j * D:(j + 1) * D], None, mlp_rows,
                                            bass.IndirectOffsetOnAxis(ap=slot[:, g * GT + j:g * GT + j + 1], axis=0),
                                            bounds_check=ST * P - 1, oob_is_err=False
                                            ).then_inc(s_yback[g % 2], 16)

            def attention(l):
                def step(i):
                    rsqrt(l, i)
                    if 0 <= i < G:
                        norm_probs(l, i)
                    if l == 1 and i + 4 < G and i >= -2:
                        gather_back(i + 4)
                each_step(l, step)

            def gather(l, s):
                if s >= 6:
                    pool.wait_ge(s_rt if l == 0 else s_yb, l * ST + s - 5)
                pool.indirect_dma_start(rows[s % 6][:, 0:(D, RW)[l]], None, tok_rows[l],
                                        bass.IndirectOffsetOnAxis(ap=src[:, s:s + 1], axis=0),
                                        bounds_check=TOK - 1, oob_is_err=False).then_inc(s_row_in[l][s % 6], 16)

            def scatter(s):
                pool.wait_ge(s_yb, ST + s + 1)
                pool.indirect_dma_start(out_rows, bass.IndirectOffsetOnAxis(ap=dst[:, s:s + 1], axis=0),
                                        ob[s % 3][:, :], None,
                                        bounds_check=TOK - 1, oob_is_err=False).then_inc(s_scat[s % 3], 16)

            for l in range(2):
                attention(l)
                pool.wait_ge(s_src, l + 1)
                for h in range(2):
                    pool.wait_ge(s_store[h], 16 * (l + 1) * (G // 2))
                for s in range(ST + 5):
                    if s < ST:
                        gather(l, s)
                    if l == 1 and s >= 5:
                        scatter(s - 5)
                if l == 0:
                    for r in range(3):
                        pool.wait_ge(s_out[r], 16 * (ST // 3))
                    gather_back(0)
                    gather_back(1)

        @block.scalar
        def _(act):
            act.dma_start(WT[0][0][:, :], t["L0_xattn_Wq"]).then_inc(s_wload[0], 16)
            act.dma_start(WT[0][1][:, :], t["L0_xattn_Wk"]).then_inc(s_wload[0], 16)
            act.dma_start(WT[0][2][:, :], t["L0_xattn_Wv"]).then_inc(s_wload[0], 16)
            for m in range(3):
                act.dma_start(WT[1][m][:, :], t[f"L1_xattn_W{'qkv'[m]}"]).then_inc(s_wload[0], 16)
            chain = [0]

            def link(ins):
                chain[0] += 1
                ins.then_inc(s_act, 1)
                act.wait_ge(s_act, chain[0])

            for l in range(2):
                act.wait_ge(s_wt, l + 1)
                for m in range(3):
                    ins = act.copy(WT[l][m][:, :], bank[l][:, m * D:(m + 1) * D])
                ins.then_inc(s_wtc, 1)
            act.wait_ge(s_small, 16 * 13)
            act.activation(tanh_g[:, :], graw[:, :], ACT.Tanh).then_inc(s_tanh, 1)
            act.wait_ge(s_gate, 1)
            link(act.activation(wg_ln[:, :], wg_ss[:, :], ACT.Ln))
            act.activation(wg_r[:, :], wg_ln[:, :], ACT.Exp, scale=-0.5).then_inc(s_gate, 1)

            def attention(l):
                def step(i):
                    a, b = i - 1, i + 1
                    if 0 <= b < G and l == 0:
                        act.wait_ge(s_cT, b + 1)
                        act.copy(ctxT[:, cols(b)], pC[:, :]).then_inc(s_cTc, 1)
                    if 0 <= b < G:
                        act.wait_ge(s_xT, n(l, b))
                        if n(l, b) > 2:
                            act.wait_ge(s_q, n(l, b) - 2)
                        act.copy(xnT[b % 2][:, :], pT[:, :]).then_inc(s_xTc, 1)
                    if 0 <= i < G:
                        act.wait_ge(s_sub, n(l, i))
                        if n(l, i) > 2:
                            act.wait_ge(s_prn, n(l, i) - 2)
                        act.activation(pr[i % 2][:, :, :], sc[i % 2][:, :, :], ACT.Exp,
                                       scale=D ** -0.5 if l == 0 else 1.0).then_inc(s_exp, 1)
                    if 0 <= b < G:
                        act.wait_ge(s_k, n(l, b))
                        act.activation(kT[b % 2][:, :], pK[:, :], ACT.Identity,
                                       bias=bias_qk[:, 2 * l + 1:2 * l + 2]).then_inc(s_kc, 1)
                        act.wait_ge(s_q, n(l, b))
                        act.activation(qT[b % 2][:, :], pQ[:, :], ACT.Identity,
                                       bias=bias_qk[:, 2 * l:2 * l + 1]).then_inc(s_qc, 1)
                    if 0 <= a < G and l == 1:
                        if a < 2:
                            act.wait_ge(s_store[a], 16 * (G // 2))
                        else:
                            act.wait_ge(s_store[a % 2], 16 * (G // 2 + a // 2))
                        act.copy(hat[a % 2][:, :, D:2 * D], tiles3(X[:, cols(a)])).then_inc(s_rowx, 1)
                    if 0 <= i < G:
                        act.wait_ge(s_pT, n(l, i))
                        if n(l, i) > 2:
                            act.wait_ge(s_pv, n(l, i) - 2)
                        pP3 = pP[0:S, :].rearrange("p (j c) -> p j c", j=GT)
                        for h in range(2):
                            part = slice(h * S, (h + 1) * S)
                            ins = act.copy(prT[i % 2][part, :, part], pP3[:, :, part])
                        ins.then_inc(s_pTc, 1)
                    if 0 <= a < G:
                        act.wait_ge(s_x2T, n(l, a))
                        if n(l, a) > 2:
                            act.wait_ge(s_lg, n(l, a) - 2)
                        act.copy(xn2T[a % 2][:, :], pT[:, :]).then_inc(s_x2Tc, 1)
                    if 0 <= a < G and l == 1:
                        act.wait_ge(s_gsub, a + 1)
                        act.activation(gs[:, :, :], gl[:, :, :], ACT.Exp).then_inc(s_gexp, 1)
                each_step(l, step)

            def mlp(l):
                func = ACT.Relu if l == 0 else ACT.Gelu

                def step(q, r):
                    q2, r2 = ahead(q, r, 2)
                    if l == 1 and valid(q2, r2):
                        act.wait_ge(s_rt, ST + num(q2, r2) + 1)
                        act.wait_ge(s_h, ST + num(q2, r2) - 2)
                        act.copy(rT[r2 % 3][:, :], pX[:, 0:P]).then_inc(s_rtc, 1)
                    if valid(q, r):
                        act.wait_ge(s_ht, l * ST + num(q, r) + 1)
                        if has_before(l, q, r, 3):
                            act.wait_ge(s_y, l * ST + num(q, r) - 2)
                        act.activation(hT[r % 3][:, :], pHT[r % 3][:, :], func).then_inc(s_hTc, 1)
                each_tile(act, 2, 0, step)

            attention(0)
            for k in range(2 * E):
                act.wait_ge(s_wt, 2 + k + 1)
                to = W1[0] if k < E else W2[0]
                act.copy(to[:, (k % E) * F:(k % E + 1) * F], bank[1 + k % 2][:, :]).then_inc(s_wtc, 1)
            act.wait_ge(s_azs, 1)
            act.activation(alpha[:, :], top[:, :], ACT.Exp, scale=-1.0).then_inc(s_aexp, 1)
            mlp(0)
            attention(1)
            mlp(1)

        @block.vector
        def _(dve):
            chain = [0]

            def link(ins):
                chain[0] += 1
                ins.then_inc(s_dve, 1)
                dve.wait_ge(s_dve, chain[0])

            dve.memset(pin[0][:, :], 1.0)
            link(dve.memset(pin[1][:, :], 1.0))
            dve.wait_ge(s_small, 16 * 13)
            link(dve.tensor_tensor(wg_sq[:, :], wg_raw[:, :], wg_raw[:, :], ALU.mult))
            link(dve.reduce_sum(wg_ss[:, :], wg_sq[:, :], X_AXIS))
            dve.tensor_scalar(wg_ss[:, :], wg_ss[:, :], GATE_EPS ** 2, None, ALU.max).then_inc(s_gate, 1)
            dve.wait_ge(s_gate, 2)
            link(dve.tensor_tensor(wg_t[:, 0:1], wg_r[:, :], wg_r[:, :], ALU.mult))
            link(dve.tensor_tensor(wg_t[:, 1:2], wg_t[:, 0:1], wg_ss[:, :], ALU.mult))
            link(dve.tensor_scalar(wg_t[:, 2:3], wg_t[:, 1:2], -0.5, 1.5, ALU.mult, ALU.add))
            link(dve.tensor_tensor(wg_t[:, 0:1], wg_t[:, 2:3], wg_r[:, :], ALU.mult))
            dve.tensor_scalar(wg_u[:, :], wg_raw[:, :], wg_t[:, 0:1], None, ALU.mult).then_inc(s_gate, 1)
            dve.wait_ge(s_gate, 4)
            dve.tensor_copy(gateT[0][:, :], bank[2][:, 0:E])
            dve.tensor_copy(ln_gT[:, :], bank[2][:, E:2 * E])
            dve.tensor_copy(ln_bT[:, :], bank[2][:, 2 * E:3 * E])
            dve.tensor_copy(wg_uT[:, :], bank[2][0:R, 3 * E:4 * E]).then_inc(s_gate, 1)
            dve.wait_ge(s_gate, 6)
            link(dve.tensor_copy(gateT[1][:, :], bank[3][:, 0:E]))
            dve.wait_ge(s_tanh, 1)
            dve.wait_ge(s_const, N_CONST)

            def stats(g, mv):
                for j in range(GT):
                    ins = dve.bn_stats(bn6[:, j, :], X[:, g * W + j * D:g * W + (j + 1) * D])
                link(ins)
                for j in range(GT):
                    ins = dve.bn_aggr(mv[g % 2][:, j, :], bn6[:, j, :])
                link(ins)

            def normed(to, g, mv, scale, wide=D):
                for j in range(GT):
                    ins = dve.tensor_scalar(to[:, j, 0:wide], X[:, g * W + j * D:g * W + (j + 1) * D],
                                            mv[g % 2][:, j, 0:1], scale[:, j:j + 1], ALU.subtract, ALU.mult)
                return ins

            def attention(l):
                def step(i):
                    a, b, c = i - 1, i + 1, i + 2
                    if 0 <= i < G:
                        dve.wait_ge(s_sc, n(l, i))
                        ps = pS[:, 0:GT * S].rearrange("p (j c) -> p j c", j=GT)
                        link(dve.reduce_max(mx[:, :], ps, X_AXIS))
                        dve.tensor_tensor(sc[i % 2][:, :, :], ps, mx[:, :].unsqueeze(2).to_broadcast([P, GT, S]),
                                          ALU.subtract).then_inc(s_sub, 1)
                    if 0 <= c < G:
                        if l == 0:
                            dve.wait_ge(s_in[c % 2], 32 * (c // 2 + 1))
                        else:
                            dve.wait_ge(s_yback[c % 2], 16 * GT * (c // 2 + 1))
                            for j in range(GT):
                                xs = X[:, c * W + j * D:c * W + (j + 1) * D]
                                ins = dve.scalar_tensor_tensor(xs, ymlp[c % 2][:, j * D:(j + 1) * D],
                                                               alpha[:, c * GT + j:c * GT + j + 1], xs,
                                                               ALU.mult, ALU.add)
                            ins.then_inc(s_stA, 1)
                            dve.wait_ge(s_stA, c + 1)
                        stats(c, mvA)
                        link(dve.tensor_scalar(pin[i % 2][:, 0:GT], mvA[c % 2][:, :, 1], EPS, None, ALU.add))
                    dve.wait_ge(s_dve, chain[0])
                    dve.engine_nop().then_inc(s_pin, 1)
                    if 0 <= b < G:
                        dve.wait_ge(s_v, n(l, b))
                        dve.tensor_tensor(v[b % 2][:, :, :], tiles3(pV[:, :]),
                                          bias_v[:, l:l + 1, :].to_broadcast([P, GT, D]), ALU.add
                                          ).then_inc(s_vc, 1)
                    if 0 <= i < G:
                        dve.wait_ge(s_exp, n(l, i))
                        link(dve.reduce_sum(den[:, :], pr[i % 2][:, :, :], X_AXIS))
                        link(dve.reciprocal(rden[:, :], den[:, :]))
                        if n(l, i) > 2:
                            dve.wait_ge(s_prn, n(l, i) - 2)
                        dve.tensor_scalar(rdg[i % 2][:, :], rden[:, :], tanh_g[:, l:l + 1], None, ALU.mult
                                          ).then_inc(s_rd, 1)
                    dve.wait_ge(s_pow, l * STEPS + i + 3)
                    if 0 <= a < G:
                        if n(l, a) > 2:
                            dve.wait_ge(s_x2T, n(l, a) - 2)
                            dve.wait_ge(s_store[a % 2], 16 * (l * (G // 2) + a // 2))
                        if l == 0:
                            normed(xn2[a % 2], a, mvB, pout[i % 2][:, GT:2 * GT]).then_inc(s_xn2, 1)
                            normed(hat[a % 2], a, mvB, pout[i % 2][:, 2 * GT:3 * GT], D).then_inc(s_row, 1)
                            dve.wait_ge(s_xn2, a + 1)
                            dve.wait_ge(s_row, a + 1)
                            dve.scalar_tensor_tensor(tiles3(X[:, cols(a)]), xn2[a % 2][:, :, :], tanh_g[:, 2:3],
                                                     tiles3(X[:, cols(a)]), ALU.mult, ALU.add).then_inc(s_x2, 1)
                        else:
                            normed(hat[a % 2], a, mvB, pout[i % 2][:, GT:2 * GT], D).then_inc(s_xn2, 1)
                    if 0 <= c < G:
                        if n(l, c) > 2:
                            dve.wait_ge(s_xT, n(l, c) - 2)
                        ins = normed(xn[c % 2], c, mvA, pout[i % 2][:, 0:GT])
                        ins.then_inc(s_xn, 1)
                        dve.wait_ge(s_xn, n(l, c))
                    elif 0 <= a < G:
                        dve.wait_ge(s_xn2, n(l, a))
                    dve.engine_nop().then_inc(s_powu, 1)
                    if 0 <= i < G:
                        dve.wait_ge(s_pv, n(l, i))
                        dve.tensor_tensor(X[:, cols(i)], X[:, cols(i)], pO[:, :], ALU.add).then_inc(s_x1, 1)
                        dve.wait_ge(s_x1, n(l, i))
                        stats(i, mvB)
                        nxt = pin[(i + 1) % 2]
                        link(dve.tensor_scalar(nxt[:, GT:2 * GT], mvB[i % 2][:, :, 1], EPS, None, ALU.add))
                        link(dve.tensor_scalar(nxt[:, 2 * GT:3 * GT], mvB[i % 2][:, :, 1], 1.0 + EPS, EPS * EPS,
                                               ALU.mult, ALU.add))
                    if 0 <= a < G:
                        dve.wait_ge(s_lg, n(l, a))
                        lg = LG[:, a * GT:(a + 1) * GT, :]
                        dve.tensor_copy(lg, pL.rearrange("p (j e) -> p j e", j=GT)).then_inc(s_lgc, 1)
                        if l == 1:
                            dve.wait_ge(s_lgc, n(l, a))
                            link(dve.reduce_max(gm[:, :], lg, X_AXIS))
                            dve.tensor_tensor(gl[:, :, :], lg, gm[:, :].unsqueeze(2).to_broadcast([P, GT, E]),
                                              ALU.subtract).then_inc(s_gsub, 1)
                            dve.wait_ge(s_gexp, a + 1)
                            link(dve.reduce_sum(gd[:, :], gs[:, :, :], X_AXIS))
                            link(dve.reciprocal(gm[:, :], gd[:, :]))
                            dve.tensor_scalar(hat[a % 2][:, :, 2 * D], gm[:, :], tanh_g[:, 3:4], None, ALU.mult
                                              ).then_inc(s_row, 1)
                each_step(l, step)

            def route(l):
                dve.wait_ge(s_lgc, n(l, G - 1))
                ins = dve.reduce_max(top[:, :], LG[:, :, :], X_AXIS)
                if l == 0:
                    ins.then_inc(s_azs, 1)
                    dve.wait_ge(s_azs, 1)
                else:
                    link(ins)
                te = [P, TILES, E]
                link(dve.tensor_tensor(hit[:, :, :], LG[:, :, :], top[:, :].unsqueeze(2).to_broadcast(te), ALU.is_equal))
                link(dve.tensor_tensor(hit[:, :, :], hit[:, :, :], iota_e[:, :].unsqueeze(1).to_broadcast(te), ALU.mult))
                link(dve.tensor_reduce(first[:, :], hit[:, :, :], X_AXIS, ALU.min))
                link(dve.tensor_tensor(oh[:, :, :].rearrange("p e t -> p t e"), first[:, :].unsqueeze(2).to_broadcast(te),
                                       iota_e[:, :].unsqueeze(1).to_broadcast(te), ALU.is_equal))
                dve.reduce_sum(cnt[:, :], oh[:, :, :], X_AXIS).then_inc(s_cnt, 1)
                link(dve.tensor_tensor_scan(cum[:, :, :].rearrange("p e t -> p (e t)"), ones_et[:, :],
                                            oh[:, :, :].rearrange("p e t -> p (e t)"), 0.0, ALU.mult, ALU.add))
                dve.wait_ge(s_pfx, l + 1)
                link(dve.tensor_scalar(tf[:, :], bank[0][:, E:2 * E], float(P - 1), None, ALU.add))
                link(dve.tensor_copy(ti[:, :], tf[:, :]))
                link(dve.tensor_scalar(ti[:, :], ti[:, :], 7, None, ALU.logical_shift_right))
                link(dve.tensor_copy(tcnt[:, :], ti[:, :]))
                link(dve.tensor_tensor_scan(tend[:, :], ones_et[:, 0:E], tcnt[:, :], 0.0, ALU.mult, ALU.add))
                link(dve.tensor_tensor(ends[:, :], tend[:, :], tcnt[:, :], ALU.subtract))
                link(dve.tensor_scalar(ends[:, :], ends[:, :], float(P), -1.0, ALU.mult, ALU.add))
                link(dve.tensor_tensor(off[:, :], ends[:, :], bank[0][:, 0:E], ALU.add))
                link(dve.tensor_tensor(ends[:, :], cum[:, :, TILES - 1], cnt[:, :], ALU.subtract))
                link(dve.tensor_tensor(off[:, :], off[:, :], ends[:, :], ALU.subtract))
                et = [P, E, TILES]
                link(dve.tensor_tensor(cum[:, :, :], cum[:, :, :], off[:, :].unsqueeze(2).to_broadcast(et), ALU.add))
                link(dve.tensor_tensor(cum[:, :, :], cum[:, :, :], oh[:, :, :], ALU.mult))
                link(dve.reduce_sum(slot_f[:, :], cum[:, :, :].rearrange("p e t -> p t e"), X_AXIS))
                link(dve.tensor_copy(slot[:, :], slot_f[:, :]))
                dve.tensor_scalar(hi_i[:, :], slot[:, :], 7, None, ALU.logical_shift_right)
                link(dve.tensor_scalar(lo_i[:, :], slot[:, :], P - 1, None, ALU.bitwise_and))
                dve.tensor_copy(hi[:, :], hi_i[:, :])
                dve.tensor_copy(lo[:, :], lo_i[:, :]).then_inc(s_hilo, 1)
                dve.wait_ge(s_hilo, l + 1)
                for tt in range(TILES):
                    if l * TILES + tt >= 4:
                        dve.wait_ge(s_invm, l * TILES + tt - 3)
                    dve.tensor_scalar(in_lo[tt % 4][:, :], iota_p[:, :], lo[:, tt:tt + 1], None, ALU.is_equal)
                    dve.tensor_scalar(in_hi[tt % 4][:, :], iota_s[:, :], hi[:, tt:tt + 1], token1[:, tt:tt + 1],
                                      ALU.is_equal, ALU.mult).then_inc(s_lo, 1)
                se = [P, ST, E]
                link(dve.tensor_tensor(ge[:, :, :], iota_s[:, :].unsqueeze(2).to_broadcast(se),
                                       tend[:, :].unsqueeze(1).to_broadcast(se), ALU.is_ge))
                link(dve.reduce_sum(eid_f[:, :], ge[:, :, :], X_AXIS))
                link(dve.tensor_scalar(eid_f[:, :], eid_f[:, :], float(E - 1), None, ALU.min))
                dve.tensor_copy(eid[:, :], eid_f[:, :]).then_inc(s_eid, 1)
                dve.wait_ge(s_invm, (l + 1) * TILES)
                link(dve.tensor_copy(inv_f[:, :], bank[3][:, 0:ST]))
                link(dve.tensor_scalar(src_f[:, :], inv_f[:, :], -1.0, 0.0, ALU.add, ALU.max))
                if l == 1:
                    link(dve.tensor_scalar(dst_f[:, :], inv_f[:, :], 0.0, EMPTY, ALU.is_equal, ALU.mult))
                    link(dve.tensor_tensor(dst_f[:, :], dst_f[:, :], src_f[:, :], ALU.add))
                    link(dve.tensor_copy(dst[:, :], dst_f[:, :]))
                dve.tensor_copy(src[:, :], src_f[:, :]).then_inc(s_src, 1)
                if l == 0:
                    dve.wait_ge(s_aexp, 1)
                    link(dve.tensor_scalar(alpha[:, :], alpha[:, :], 1.0, None, ALU.add))
                    link(dve.reciprocal(alpha[:, :], alpha[:, :]))
                    link(dve.tensor_scalar(alpha[:, :], alpha[:, :], tanh_g[:, 2:3], None, ALU.mult))

            def mlp(l):
                base = l * ST
                dve.wait_ge(s_eid, l + 1)
                dve.wait_ge(s_wload[3], 48 + 16 * l)

                def expert(q, r):
                    return dve.value_load(eid[0:1, bass.ds(num(q, r), 1)], min_val=0, max_val=E - 1)

                def step(q, r):
                    q2, r2 = ahead(q, r, 2)
                    q1, r1 = ahead(q, r, 1)
                    q0, rp = ahead(q, r, -1)
                    if l == 0 and valid(q2, r2):
                        ev = expert(q2, r2)
                        dve.wait_ge(s_rt, num(q2, r2) + 1)
                        if has_before(0, q2, r2, 3):
                            dve.wait_ge(s_h, num(q2, r2) - 2)
                        dve.tensor_scalar(rT[r2 % 3][:, :], pX[:, 0:P], ln_gT[:, bass.ds(ev, 1)],
                                          ln_bT[:, bass.ds(ev, 1)], ALU.mult, ALU.add).then_inc(s_rtc, 1)
                    if valid(q1, r1):
                        ev = expert(q1, r1)
                        dve.wait_ge(s_h, base + num(q1, r1) + 1)
                        if has_before(l, q1, r1, 3):
                            dve.wait_ge(s_ht, base + num(q1, r1) - 2)
                        dve.tensor_tensor(hb[r1 % 3][:, :], pH[r1 % 3][:, :], B1[:, bass.ds(ev * F, F)], ALU.add
                                          ).then_inc(s_hb, 1)
                    if valid(q0, rp):
                        ev = expert(q0, rp)
                        dve.wait_ge(s_y, base + num(q0, rp) + 1)
                        if l == 0:
                            if has_before(0, q0, rp, 3):
                                dve.wait_ge(s_out[rp % 3], 16 * third(q0, rp))
                            dve.tensor_tensor(yb[rp % 3][:, :], pY[:, 0:D], B2[l][:, bass.ds(ev * D, D)], ALU.add
                                              ).then_inc(s_yb, 1)
                        else:
                            if has_before(0, q0, rp, 3):
                                dve.wait_ge(s_scat[rp % 3], 16 * third(q0, rp))
                            link_y(dve.tensor_tensor(yb[rp % 3][:, :], pY[:, 0:D], B2[l][:, bass.ds(ev * D, D)], ALU.add),
                                   num(q0, rp) + 1)
                            dve.scalar_tensor_tensor(ob[rp % 3][:, :], yb[rp % 3][:, :], rows[rp][:, 2 * D:2 * D + 1],
                                                     rows[rp][:, D:2 * D], ALU.mult, ALU.add).then_inc(s_yb, 1)

                def link_y(ins, value):
                    ins.then_inc(s_y1, 1)
                    dve.wait_ge(s_y1, value)
                each_tile(dve, 2, 1, step)

            attention(0)
            route(0)
            mlp(0)
            attention(1)
            route(1)
            mlp(1)

        @block.tensor
        def _(pe):
            pe.wait_ge(s_const, N_CONST)
            pe.wait_ge(s_wload[0], 96)
            for l in range(2):
                for m in range(3):
                    ins = pe.transpose(bank[l][:, m * D:(m + 1) * D], WT[l][m][:, :], ident[:, :])
                ins.then_inc(s_wt, 1)
            pe.wait_ge(s_small, 16 * 13)
            pe.wait_ge(s_gate, 3)
            for m in range(3):
                pe.transpose(bank[2][:, m * E:(m + 1) * E], raw_small[:, m, :], ident[0:E, 0:E])
            pe.transpose(bank[2][0:R, 3 * E:4 * E], wg_u[:, :], ident[0:E, 0:E]).then_inc(s_gate, 1)
            pe.wait_ge(s_gate, 5)
            pe.matmul(bank[3][:, 0:E], wg_red[:, :], wg_uT[:, :], start=True, stop=True).then_inc(s_gate, 1)
            pe.wait_ge(s_gate, 6)
            pe.wait_ge(s_wtc, 2)

            def tile_of(ap, j, w=D):
                return ap[:, j * w:(j + 1) * w]

            def attention(l):
                wq, wk, wv = (w[:, :] for w in WT[l])

                def step(i):
                    a, b = i - 1, i + 1
                    if 0 <= i < G:
                        pe.wait_ge(s_kc, n(l, i))
                        pe.wait_ge(s_qc, n(l, i))
                        if n(l, i) > 1:
                            pe.wait_ge(s_sub, n(l, i) - 1)
                            pe.wait_ge(s_lgc, l * G if i < 2 else n(l, i) - 2) if n(l, i) > 2 else None
                        for j in range(GT):
                            for h in range(2):
                                c = j * P + h * S
                                ins = pe.matmul(pS[h * S:(h + 1) * S, j * S:(j + 1) * S], qT[i % 2][:, c:c + S],
                                                kT[i % 2][:, c:c + S], start=True, stop=True)
                        ins.then_inc(s_sc, 1)
                    if 0 <= b < G and l == 0:
                        pe.wait_ge(s_in[b % 2], 32 * (b // 2 + 1))
                        if b >= 1:
                            pe.wait_ge(s_cTc, b)
                        for j in range(GT):
                            ins = pe.transpose(tile_of(pC, j), ctx_raw[b % 2][:, j, :], ident[:, :])
                        ins.then_inc(s_cT, 1)
                    if 0 <= b < G:
                        pe.wait_ge(s_xn, n(l, b))
                        if n(l, b) > 1:
                            pe.wait_ge(s_xTc, n(l, b) - 1)
                            if b >= 3 or l == 1:
                                pe.wait_ge(s_x2Tc, n(l, b - 3) if b >= 3 else G)
                        for j in range(GT):
                            ins = pe.transpose(tile_of(pT, j), xn[b % 2][:, j, :], ident[:, :])
                        ins.then_inc(s_xT, 1)
                        cT = ctxT[:, cols(b)]
                        if l == 0:
                            pe.wait_ge(s_cTc, b + 1)
                        if n(l, b) > 1:
                            pe.wait_ge(s_kc, n(l, b) - 1)
                            pe.wait_ge(s_vc, n(l, b) - 1)
                        pe.matmul(pK[:, :], wk, cT, start=True, stop=True).then_inc(s_k, 1)
                        for j in range(GT):
                            ins = pe.matmul(tile_of(pV, j), tile_of(cT, j), wv, start=True, stop=True)
                        ins.then_inc(s_v, 1)
                        pe.wait_ge(s_xTc, n(l, b))
                        if n(l, b) > 1:
                            pe.wait_ge(s_qc, n(l, b) - 1)
                        pe.matmul(pQ[:, :], wq, xnT[b % 2][:, :], start=True, stop=True).then_inc(s_q, 1)
                    if 0 <= i < G:
                        pe.wait_ge(s_prn, n(l, i))
                        if n(l, i) > 1:
                            pe.wait_ge(s_pTc, n(l, i) - 1)
                        for j in range(GT):
                            ins = pe.transpose(pP[0:S, j * P:(j + 1) * P], prn[i % 2][:, j, :], ident[:, :])
                        ins.then_inc(s_pT, 1)
                    if 0 <= a < G:
                        pe.wait_ge(s_xn2, n(l, a))
                        pe.wait_ge(s_xTc, n(l, min(b, G - 1)))
                        xs = xn2 if l == 0 else hat
                        for j in range(GT):
                            ins = pe.transpose(tile_of(pT, j), xs[a % 2][:, j, 0:D], ident[:, :])
                        ins.then_inc(s_x2T, 1)
                    if 0 <= i < G:
                        pe.wait_ge(s_pTc, n(l, i))
                        pe.wait_ge(s_vc, n(l, i))
                        if n(l, i) > 1:
                            pe.wait_ge(s_x1, n(l, i) - 1)
                        for j in range(GT):
                            ins = pe.matmul(tile_of(pO, j), prT[i % 2][:, j, :], v[i % 2][:, j, :],
                                            start=True, stop=True)
                        ins.then_inc(s_pv, 1)
                    if 0 <= a < G:
                        pe.wait_ge(s_x2Tc, n(l, a))
                        if n(l, a) > 1:
                            pe.wait_ge(s_lgc, n(l, a) - 1)
                        if i < G:
                            pe.wait_ge(s_sub, n(l, i))
                        for j in range(GT):
                            ins = pe.matmul(tile_of(pL, j, E), tile_of(xn2T[a % 2], j), gateT[l][:, :],
                                            start=True, stop=True)
                        ins.then_inc(s_lg, 1)
                each_step(l, step)

            def route(l):
                pe.wait_ge(s_cnt, l + 1)
                pe.matmul(bank[0][:, 0:E], before[:, :], cnt[:, :], start=True, stop=True)
                pe.matmul(bank[0][:, E:2 * E], ones[:, :], cnt[:, :], start=True, stop=True).then_inc(s_pfx, 1)
                if l == 0:
                    pe.wait_ge(s_wload[1], 16)
                    pe.wait_ge(s_wload[2], 16)
                    for k in range(2 * E):
                        if k >= 2:
                            pe.wait_ge(s_wtc, 2 + k - 1)
                        raw = W1[1] if k < E else W2[1]
                        for c in range(FC):
                            col = (k % E) * F + c * P
                            ins = pe.transpose(bank[1 + k % 2][:, c * P:(c + 1) * P], raw[:, col:col + P], ident[:, :])
                        ins.then_inc(s_wt, 1)
                for tt in range(TILES):
                    pe.wait_ge(s_lo, l * TILES + tt + 1)
                    pe.matmul(bank[3][:, 0:ST], in_lo[tt % 4][:, :], in_hi[tt % 4][:, :],
                              start=(tt == 0), stop=(tt == TILES - 1)).then_inc(s_invm, 1)
                if l == 0:
                    pe.wait_ge(s_wtc, 2 + 2 * E)
                else:
                    pe.wait_ge(s_l1w, 32)

            def mlp(l):
                base = l * ST
                pe.wait_ge(s_eid, l + 1)
                pe.wait_ge(s_src, l + 1)

                def expert(q, r):
                    return pe.value_load(eid[0:1, bass.ds(num(q, r), 1)], min_val=0, max_val=E - 1)

                def step(q, r):
                    q2, r2 = ahead(q, r, 2)
                    q1, r1 = ahead(q, r, 1)
                    q0, rp = ahead(q, r, -1)
                    if valid(q2, r2):
                        pe.wait_ge(s_row_in[l][r2], 16 * (q2 + 1))
                        if has_before(l, q2, r2, 1):
                            pe.wait_ge(s_rtc, base + num(q2, r2))
                        pe.transpose(pX[:, 0:P], rows[r2][:, 0:D], ident[:, :]).then_inc(s_rt, 1)
                    if valid(q1, r1):
                        ev = expert(q1, r1)
                        pe.wait_ge(s_rtc, base + num(q1, r1) + 1)
                        if has_before(l, q1, r1, 3):
                            pe.wait_ge(s_hb, base + num(q1, r1) - 2)
                        pe.matmul(pH[r1 % 3][:, :], rT[r1 % 3][:, :], W1[l][:, bass.ds(ev * F, F)],
                                  start=True, stop=True).then_inc(s_h, 1)
                    if valid(q, r):
                        pe.wait_ge(s_hb, base + num(q, r) + 1)
                        if has_before(l, q, r, 3):
                            pe.wait_ge(s_hTc, base + num(q, r) - 2)
                        for c in range(FC):
                            ins = pe.transpose(pHT[r % 3][:, c * P:(c + 1) * P], hb[r % 3][:, c * P:(c + 1) * P], ident[:, :])
                        ins.then_inc(s_ht, 1)
                    if valid(q0, rp):
                        ev = expert(q0, rp)
                        pe.wait_ge(s_hTc, base + num(q0, rp) + 1)
                        if has_before(l, q0, rp, 1):
                            pe.wait_ge(s_yb, base + num(q0, rp))
                        for c in range(FC):
                            ins = pe.matmul(pY[:, 0:D], hT[rp % 3][:, c * P:(c + 1) * P],
                                            W2[l][:, bass.ds(ev * F + c * P, P)],
                                            start=(c == 0), stop=(c == FC - 1))
                        ins.then_inc(s_y, 1)
                each_tile(pe, 2, 1, step)

            attention(0)
            route(0)
            mlp(0)
            attention(1)
            route(1)
            mlp(1)


_INS = ["x", "ctx_1024", "g_xattn", "g_ffn",
        "L0_xattn_Wq", "L0_xattn_bq", "L0_xattn_Wk", "L0_xattn_bk", "L0_xattn_Wv", "L0_xattn_bv",
        "L0_ffn_centroids", "L0_ffn_ln_g", "L0_ffn_ln_b", "L0_ffn_w1", "L0_ffn_b1", "L0_ffn_w2", "L0_ffn_b2",
        "L1_xattn_Wq", "L1_xattn_bq", "L1_xattn_Wk", "L1_xattn_bk", "L1_xattn_Wv", "L1_xattn_bv",
        "L1_ffn_wg_red", "L1_ffn_wg", "L1_ffn_w1", "L1_ffn_b1", "L1_ffn_w2", "L1_ffn_b2"]


def kernel(**inputs):
    import numpy as _np
    import concourse.bacc as _bacc
    from concourse import mybir as _mybir
    from concourse.bass_utils import run_bass_kernel_spmd as _run

    nc = _bacc.Bacc("TRN2", target_bir_lowering=False, num_devices=1)
    arrays, args = {}, {}
    for name in _INS:
        a = _np.ascontiguousarray(inputs[name])
        arrays[f"in_{name}_dram"] = a
        args[name] = nc.dram_tensor(f"in_{name}_dram", a.shape, _mybir.dt.from_np(a.dtype), kind="ExternalInput").ap()
    out = nc.dram_tensor("out_0_dram", tuple(inputs["x"].shape), _mybir.dt.float32, kind="ExternalOutput").ap()
    build(nc, args, out)
    r = _run(nc, [arrays], core_ids=[0])
    return r.results[0]["out_0_dram"]
```

```python
from contextlib import ExitStack

import concourse.bass as bass
from concourse import mybir

F32 = mybir.dt.float32
F32R = mybir.dt.float32r
BF16 = mybir.dt.bfloat16
I32 = mybir.dt.int32
ALU = mybir.AluOpType
ACT = mybir.ActivationFunctionType
X_AXIS = mybir.AxisListType.X

P = 128
EPS = 1e-5
GATE_EPS = 1e-4
EMPTY = 8192.0


def build(nc, t, out):
    B, S, D = t["x"].shape
    E, F, _ = t["L0_ffn_w1"].shape
    R = t["L1_ffn_wg_red"].shape[0]
    TOK = B * S
    TILES = TOK // P
    GT = 4
    G = TILES // GT
    W = GT * D
    FC = F // P
    ST = TILES + E - 1
    U = 12
    TURNS = -(-ST // U)
    WIN = 16
    RW = 2 * D + 4
    assert D == P and S * 2 == P and ST % 3 == 0 and P // 2 == S

    x_rows = t["x"].rearrange("b s d -> (b s) d")
    ctx_rows = t["ctx_1024"].rearrange("b s d -> (b s) d")
    out_rows = out.rearrange("b s d -> (b s) d")
    tok_rows = [nc.dram_tensor("tok_rows0", [TOK, D], F32, kind="Internal").ap(),
                nc.dram_tensor("tok_rows1", [TOK, RW], F32, kind="Internal").ap()]
    mlp_rows = nc.dram_tensor("mlp_rows", [ST * P, D], F32, kind="Internal").ap()

    with ExitStack() as ctx:
        def sb(name, shape, dt=F32):
            return ctx.enter_context(nc.sbuf_tensor(name, shape, dt))

        def sem(name):
            return ctx.enter_context(nc.semaphore(name))

        def tiles3(ap):
            return ap.rearrange("p (j d) -> p j d", j=GT)

        X = sb("X", [P, TOK])
        ctxT = sb("ctxT", [P, TOK])
        WT = [[sb(f"WT{l}{m}", [P, D]) for m in "qkv"] for l in range(2)]
        bias_qk = sb("bias_qk", [P, 4])
        bias_v = sb("bias_v", [P, 2, D])
        W1 = [sb(f"W1_{l}", [P, E * F]) for l in range(2)]
        W2 = [sb(f"W2_{l}", [P, E * F]) for l in range(2)]
        B1 = sb("B1", [P, E * F])
        B2 = [sb(f"B2_{l}", [P, E * D]) for l in range(2)]
        ln_gT, ln_bT = sb("ln_gT", [P, E]), sb("ln_bT", [P, E])
        gateT = [sb("gateT0", [P, E]), sb("gateT1", [P, E])]
        tanh_g = sb("tanh_g", [P, 4])
        ident, ones = sb("ident", [P, P]), sb("ones", [P, P])
        before = sb("before", [P, P])
        iota_e = sb("iota_e", [P, E])
        iota_p = sb("iota_p", [P, P])
        iota_s = sb("iota_s", [P, ST])
        iota_w = sb("iota_w", [P, TURNS, WIN])
        tile1 = sb("tile1", [P, TILES])
        own_p = sb("own_p", [P, 1])

        raw_small = sb("raw_small", [E, 3, D])
        wg_raw, wg_red = sb("wg_raw", [E, R]), sb("wg_red", [R, D])
        wg_sq, wg_ss = sb("wg_sq", [E, R]), sb("wg_ss", [E, 1])
        wg_r, wg_u = sb("wg_r", [E, 1]), sb("wg_u", [E, R])
        wg_uT = sb("wg_uT", [R, E])
        graw = sb("graw", [P, 4])

        shared = sb("shared", [P, E * F])
        shared_part = [shared[:, k * F:(k + 1) * F] for k in range(E)]
        ctx_raw = [tiles3(b) for b in shared_part[0:2]]
        ymlp = shared_part[2:4]
        prT = [tiles3(b) for b in shared_part[4:6]]
        xn2T = shared_part[6:8]
        xn = [sb(f"xn{i}", [P, GT, D]) for i in range(2)]
        xnT = [sb(f"xnT{i}", [P, W]) for i in range(2)]
        qT = [sb(f"qT{i}", [P, W]) for i in range(2)]
        kT = [sb(f"kT{i}", [P, W]) for i in range(2)]
        v = [sb(f"v{i}", [P, GT, D]) for i in range(2)]
        pr = [sb(f"pr{i}", [P, GT, S]) for i in range(2)]
        prn = [sb(f"prn{i}", [P, GT, S]) for i in range(2)]
        xn2 = [sb(f"xn2{i}", [P, GT, D]) for i in range(2)]
        hat = [sb(f"hat{i}", [P, GT, D + 4]) for i in range(3)]
        bn6 = sb("bn6", [P, GT, 6])
        mvA = [sb(f"mvA{i}", [P, GT, 2]) for i in range(2)]
        mvB = [sb(f"mvB{i}", [P, GT, 2]) for i in range(2)]
        pin = [sb(f"pin{i}", [P, 3 * GT]) for i in range(2)]
        pout = [sb(f"pout{i}", [P, 3 * GT]) for i in range(2)]
        minus_half = sb("minus_half", [P, 3 * GT])
        nmA = [sb(f"nmA{i}", [P, GT]) for i in range(2)]
        nmB = [sb(f"nmB{i}", [P, GT]) for i in range(2)]
        mx, nmx, rden = sb("mx", [P, GT]), sb("nmx", [P, GT]), sb("rden", [P, GT])
        den = [sb(f"den{i}", [P, GT]) for i in range(2)]
        rdg = [sb(f"rdg{i}", [P, GT]) for i in range(2)]

        LG = sb("LG", [P, TILES, E])
        top = sb("top", [P, TILES])
        alpha = sb("alpha", [P, TILES])
        gl, gs = sb("gl", [P, GT, E]), sb("gs", [P, GT, E])
        gm, gd = sb("gm", [P, GT]), sb("gd", [P, GT])
        hit = sb("hit", [P, TILES, E])
        first = sb("first", [P, TILES])
        oh = sb("oh", [P, E, TILES])
        cum = sb("cum", [P, E, TILES])
        ones_et = sb("ones_et", [P, E * TILES])
        cnt, ends = sb("cnt", [P, E]), sb("ends", [P, E])
        tf, ti = sb("tf", [P, E]), sb("ti", [P, E], I32)
        tcnt, tend, off = sb("tcnt", [P, E]), sb("tend", [P, E]), sb("off", [P, E])
        slot_f = sb("slot_f", [P, TILES])
        slot = sb("slot", [P, TILES], I32)
        hi_i, lo_i = sb("hi_i", [P, TILES], I32), sb("lo_i", [P, TILES], I32)
        hi, lo = sb("hi", [P, TILES]), sb("lo", [P, TILES])
        HT = 8
        in_lo = [sb(f"in_lo{i}", [P, GT, P], BF16) for i in range(G)]
        in_hi = [sb(f"in_hi{i}", [P, 2, HT, ST], BF16) for i in range(TILES // HT)]
        eq_hi = [b[:, :, :].rearrange("p j d -> p (j d)")[:, 0:HT * ST].rearrange("p (j s) -> p j s", j=HT)
                 for b in (*xn, *xn2)]
        ge = sb("ge", [1, TURNS * WIN, E])
        eid_f, eid = sb("eid_f", [1, TURNS * WIN]), sb("eid", [1, TURNS * WIN], I32)
        inv_f, src_f, dst_f = sb("inv_f", [P, 2 * ST]), sb("src_f", [P, ST]), sb("dst_f", [P, ST])
        src, dst = sb("src", [P, ST], I32), sb("dst", [P, ST], I32)

        rows = [b[:, :, :].rearrange("p j d -> p (j d)") for b in (*v, *xn, *xn2)]
        halves = [b[:, :, :].rearrange("p j c -> p (j c)")[:, h * P:(h + 1) * P] for b in (*pr, *prn) for h in range(2)]
        rT, yb = halves[0:3], halves[3:6]
        ob = [*halves[6:8], sb("ob2", [P, D])]
        rT_hi = [sb(f"rT_hi{i}", [P, P], F32R) for i in range(3)]
        rT_lo = [sb(f"rT_lo{i}", [P, P], F32R) for i in range(3)]
        W1_hi = shared[:, :].bitcast(F32R)
        W1_lo = [w[:, :].bitcast(F32R) for w in W1]
        hb = [qT[0], qT[1], kT[0]]
        hT = [kT[1], xnT[0], xnT[1]]

        bank = [ctx.enter_context(nc.psum_tensor(f"bank{i}", [P, 512], F32)) for i in range(8)]
        pC, pS, pT, pK, pV, pP, pQ, pO = bank
        pL = pS[:, GT * S:GT * S + GT * E]
        pX, pH, pHT, pY = bank[0], bank[1:4], bank[4:7], bank[7]

        s_const = sem("s_const")
        s_wload = [sem(f"s_wload{i}") for i in range(5)]
        s_ident = sem("s_ident")
        s_bias = sem("s_bias")
        s_small = sem("s_small")
        s_l1w = sem("s_l1w")
        s_wt = sem("s_wt")
        s_wtc = sem("s_wtc")
        s_gate = sem("s_gate")
        s_tanh = sem("s_tanh")
        s_in = [sem(f"s_in{i}") for i in range(2)]
        s_cT, s_cTc = sem("s_cT"), sem("s_cTc")
        s_stA, s_pin, s_pow = sem("s_stA"), sem("s_pin"), sem("s_pow")
        s_xn, s_xT, s_xTc = sem("s_xn"), sem("s_xT"), sem("s_xTc")
        s_q, s_qc, s_k, s_kc, s_v, s_vc = (sem(n) for n in ("s_q", "s_qc", "s_k", "s_kc", "s_v", "s_vc"))
        s_sc, s_max, s_exp, s_rd, s_prn = (sem(n) for n in ("s_sc", "s_max", "s_exp", "s_rd", "s_prn"))
        s_nm, s_nmB = sem("s_nm"), sem("s_nmB")
        s_hat, s_hat_pool = sem("s_hat"), sem("s_hat_pool")
        s_pT, s_pTc, s_pv, s_x1 = (sem(n) for n in ("s_pT", "s_pTc", "s_pv", "s_x1"))
        s_xn2, s_x2T, s_x2Tc, s_lg, s_lgc = (sem(n) for n in ("s_xn2", "s_x2T", "s_x2Tc", "s_lg", "s_lgc"))
        s_gsub, s_gexp, s_score = sem("s_gsub"), sem("s_gexp"), sem("s_score")
        s_store = [sem(f"s_store{i}") for i in range(3)]
        s_yback = [sem(f"s_yback{i}") for i in range(2)]
        s_x2 = sem("s_x2")
        s_dve = sem("s_dve")
        s_eqhi, s_inhi, s_inhi_p = sem("s_eqhi"), sem("s_inhi"), sem("s_inhi_p")
        s_cnt, s_pfx, s_hilo, s_lo, s_invm, s_src, s_eid = (
            sem(n) for n in ("s_cnt", "s_pfx", "s_hilo", "s_lo", "s_invm", "s_src", "s_eid"))
        s_aexp, s_azs = sem("s_aexp"), sem("s_azs")
        s_row_in = [[sem(f"s_row_in{l}{i}") for i in range(6)] for l in range(2)]
        s_whi, s_wlo = sem("s_whi"), sem("s_wlo")
        s_rhi, s_rlo = sem("s_rhi"), sem("s_rlo")
        s_zero = sem("s_zero")
        s_rt, s_rtc, s_h, s_hb, s_ht, s_hTc, s_y, s_yb = (
            sem(n) for n in ("s_rt", "s_rtc", "s_h", "s_hb", "s_ht", "s_hTc", "s_y", "s_yb"))
        s_out = [sem(f"s_out{i}") for i in range(3)]
        s_scat = [sem(f"s_scat{i}") for i in range(3)]
        s_y1 = sem("s_y1")
        N_CONST = 16
        POWS = G + 3

        block = ctx.enter_context(nc.Block())

        def n(l, g):
            return l * G + g + 1

        def cols(g):
            return slice(g * W, (g + 1) * W)

        def each_step(l, step):
            for i in range(-2, G + 3):
                step(i)

        def wait_group(eng, semaphore, l, g):
            if n(l, g) >= 1:
                eng.wait_ge(semaphore, n(l, g))

        def stored_rows(l, slot):
            return len(range(slot, G, 3)) * (16, 48)[l]

        def waits_stored(eng, l, z):
            stored = z // 3 * 16 if l == 0 else stored_rows(0, z % 3) + z // 3 * 32
            if stored:
                eng.wait_ge(s_store[z % 3], stored)

        def each_tile(eng, lead, tail, step, with_experts=False):
            experts = load_experts(eng, 0) if with_experts else None
            for s in range(-lead, U):
                step(s // U, s % U, lambda k: experts[s + k + 1])
            with eng.Fori(1, ST // U) as q:
                experts_q = load_experts(eng, q) if with_experts else None
                for r in range(U):
                    step(q, r, lambda k: experts_q[r + k + 1])
            last = ST // U
            experts = load_experts(eng, last) if with_experts else None
            for s in range(last * U, ST + tail):
                step(s // U, s % U, lambda k: experts[s - last * U + k + 1])

        def ahead(q, r, k):
            return q + (r + k) // U, (r + k) % U

        def num(q, r):
            return U * q + r

        def load_experts(eng, q):
            return nc.values_load_multi_w_load_instructions(
                eid[0:1, bass.ds(q * WIN, WIN)], engines=[eng.engine], min_val=0, max_val=E - 1,
                skip_runtime_bounds_check_because="route() counts at most E - 1 ends, clamped by a min")[1]

        def third(q, r):
            return U // 3 * q + r // 3

        def valid(q, r):
            return not isinstance(q, int) or 0 <= num(q, r) < ST

        def has_before(l, q, r, k):
            return l == 1 or not isinstance(q, int) or num(q, r) >= k

        @block.sync
        def _(sp):
            def load_group(g):
                for dst_ap, rows_ap in ((tiles3(X[:, cols(g)]), x_rows), (ctx_raw[g % 2], ctx_rows)):
                    sp.dma_start(dst_ap, rows_ap[g * GT * P:(g + 1) * GT * P, :].rearrange("(j p) d -> p j d", p=P)
                                 ).then_inc(s_in[g % 2], 16)

            load_group(0)
            for l in range(2):
                for m in range(2):
                    sp.dma_start(bias_qk[:, 2 * l + m:2 * l + m + 1],
                                 t[f"L{l}_xattn_b{'qk'[m]}"].rearrange("(p o) -> p o", o=1)).then_inc(s_bias, 16)
            load_group(1)
            for l in range(2):
                sp.dma_start(bias_v[:, l, :], t[f"L{l}_xattn_bv"].partition_broadcast(P)).then_inc(s_bias, 16)
            sp.dma_start(graw[:, 0:2], t["g_xattn"].partition_broadcast(P)).then_inc(s_bias, 16)
            sp.dma_start(graw[:, 2:4], t["g_ffn"].partition_broadcast(P)).then_inc(s_bias, 16)
            for m, name in enumerate(("centroids", "ln_g", "ln_b")):
                sp.dma_start(raw_small[:, m, :], t[f"L0_ffn_{name}"]).then_inc(s_small, 16)
            sp.dma_start(wg_raw[:, :], t["L1_ffn_wg"]).then_inc(s_small, 16)
            sp.dma_start(wg_red[:, :], t["L1_ffn_wg_red"]).then_inc(s_small, 16)
            def store_rows(l, g):
                sp.wait_ge(s_hat, n(l, g))
                if l == 0:
                    sp.wait_ge(s_hat_pool, g + 1)
                sp.wait_ge(s_xn2, n(l, g))
                to = tok_rows[l][g * GT * P:(g + 1) * GT * P, :].rearrange("(j p) d -> p j d", p=P)
                if l == 0:
                    sp.dma_start(to, hat[g % 3][:, :, 0:D]).then_inc(s_store[g % 3], 16)
                else:
                    sp.wait_ge(s_score, g + 1)
                    sp.dma_start(to[:, :, 0:D + 4], hat[g % 3][:, :, :]).then_inc(s_store[g % 3], 16)
                    sp.dma_start(to[:, :, D + 4:RW], tiles3(X[:, cols(g)])).then_inc(s_store[g % 3], 16)

            for g in range(2, G + 6):
                if g < G:
                    sp.wait_ge(s_cT, g - 1)
                    load_group(g)
                if g == 5:
                    sp.dma_start(W1[1][:, :].rearrange("p (e c d) -> p e c d", e=E, c=FC),
                                 t["L0_ffn_w1"].rearrange("e (c p) d -> p e c d", p=P)).then_inc(s_wload[1], 16)
                if g == 6:
                    sp.dma_start(W2[1][:, :].rearrange("p (e f) -> p e f", e=E),
                                 t["L0_ffn_w2"].rearrange("e p f -> p e f")).then_inc(s_wload[2], 16)
                if g == 7:
                    sp.dma_start(B1[:, :], t["L0_ffn_b1"].rearrange("e f -> (e f)").partition_broadcast(P)
                                 ).then_inc(s_wload[3], 16)
                    for l in range(2):
                        sp.dma_start(B2[l][:, :], t[f"L{l}_ffn_b2"].rearrange("e d -> (e d)").partition_broadcast(P)
                                     ).then_inc(s_wload[3], 16)
                if g >= 6:
                    store_rows(0, g - 6)
            sp.wait_ge(s_wt, 2 + 2 * E)
            sp.dma_start(W1[1][:, :].rearrange("p (e f) -> p e f", e=E),
                         t["L1_ffn_w1"].rearrange("e d f -> d e f")).then_inc(s_l1w, 16)
            sp.dma_start(W2[1][:, :].rearrange("p (e c d) -> p e c d", e=E, c=FC),
                         t["L1_ffn_w2"].rearrange("e (c p) d -> p e c d", p=P)).then_inc(s_l1w, 16)

            def store_mlp(q, r, _):
                q, r = ahead(q, r, -1)
                if not valid(q, r):
                    return
                sp.wait_ge(s_yb, num(q, r) + 1)
                sp.dma_start(mlp_rows[bass.ds((num(q, r)) * P, P), :], yb[r % 3][:, :]).then_inc(s_out[r % 3], 16)

            each_tile(sp, 0, 1, store_mlp)
            sp.wait_ge(s_hb, ST)
            sp.dma_start(B1[:, :], t["L1_ffn_b1"].rearrange("e f -> (e f)").partition_broadcast(P)
                         ).then_inc(s_wload[3], 16)
            for g in range(G):
                store_rows(1, g)
            for r in range(3):
                sp.wait_ge(s_scat[r], 16 * (ST // 3))

        @block.gpsimd
        def _(pool):
            pool.memset(ident[:, :], 0.0).then_inc(s_ident, 1)
            pool.memset(minus_half[:, :], -0.5).then_inc(s_const, 1)
            pool.wait_ge(s_ident, 1)
            pool.affine_select(out=ident[:, :], in_=ident[:, :], compare_op=ALU.not_equal, fill=1.0, base=0,
                               pattern=[[-1, P]], channel_multiplier=1).then_inc(s_ident, 1)
            pool.wait_ge(s_const, 1)

            def rsqrt(l, i):
                pool.wait_ge(s_pin, l * POWS + i + 3)
                wait_group(pool, s_xn, l, min(i, G - 1))
                wait_group(pool, s_hat, l, i - 3)
                wait_group(pool, s_hat_pool, 0, i - 3 if l == 0 else G - 1)
                wait_group(pool, s_xn2, l, i - 3)
                used = slice(GT if i >= G - 2 else 0, (GT if i < 1 else 3 * GT if l == 0 else 2 * GT))
                pool.tensor_tensor(pout[i % 2][:, used], pin[i % 2][:, used], minus_half[:, used], ALU.pow
                                   ).then_inc(s_pow, 1)

            rsqrt(0, -2)
            pool.memset(before[:, :], 1.0).then_inc(s_const, 1)
            pool.memset(ones[:, :], 1.0).then_inc(s_const, 1)
            pool.iota(iota_e[:, :], [[1, E]], base=-E, channel_multiplier=0,
                      allow_small_or_imprecise_dtypes=True).then_inc(s_const, 1)
            pool.iota(iota_p[:, :], [[1, P]], base=0, channel_multiplier=0,
                      allow_small_or_imprecise_dtypes=True).then_inc(s_const, 1)
            pool.iota(iota_s[:, :], [[1, ST]], base=0, channel_multiplier=0,
                      allow_small_or_imprecise_dtypes=True).then_inc(s_const, 1)
            pool.iota(iota_w[:, :, :], [[U, TURNS], [1, WIN]], base=-1, channel_multiplier=0,
                      allow_small_or_imprecise_dtypes=True).then_inc(s_const, 1)
            pool.iota(tile1[:, :], [[1, TILES]], base=1, channel_multiplier=0,
                      allow_small_or_imprecise_dtypes=True).then_inc(s_const, 1)
            pool.iota(own_p[:, :], [[0, 1]], base=0, channel_multiplier=1,
                      allow_small_or_imprecise_dtypes=True).then_inc(s_const, 1)
            pool.memset(ones_et[:, :], 1.0).then_inc(s_const, 1)
            pool.wait_ge(s_const, 10)
            pool.affine_select(out=before[:, :], in_=before[:, :], compare_op=ALU.is_gt, fill=0.0, base=0,
                               pattern=[[1, P]], channel_multiplier=-1).then_inc(s_const, 1)
            pool.memset(prT[0], 0.0).then_inc(s_const, 1)
            for h in range(3):
                pool.memset(hat[h][:, :, D:D + 4], 0.0).then_inc(s_const, 1)
            pool.memset(prT[1], 0.0).then_inc(s_const, 1)
            pool.wait_ge(s_gate, 1)
            pool.tensor_tensor(wg_r[:, :], wg_ss[:, :], minus_half[0:E, 0:1], ALU.pow).then_inc(s_gate, 1)

            def norm_probs(l, g):
                pool.wait_ge(s_exp, n(l, g))
                pool.wait_ge(s_rd, n(l, g))
                if n(l, g) > 2:
                    pool.wait_ge(s_pT, n(l, g) - 2)
                pool.tensor_tensor(prn[g % 2][:, :, :], pr[g % 2][:, :, :],
                                   rdg[g % 2][:, :].unsqueeze(2).to_broadcast([P, GT, S]), ALU.mult
                                   ).then_inc(s_prn, 1)

            def mlp_norm(i):
                z = i - 2
                waits_stored(pool, 0, z)
                pool.wait_ge(s_pow, i + 2)
                for j in range(GT - 1):
                    ins = pool.tensor_scalar(hat[z % 3][:, j, 0:D], X[:, z * W + j * D:z * W + (j + 1) * D],
                                             mvB[z % 2][:, j, 0:1], pout[(i - 1) % 2][:, 2 * GT + j:2 * GT + j + 1],
                                             ALU.subtract, ALU.mult)
                ins.then_inc(s_hat_pool, 1)

            def gather_back(g):
                if g >= 2:
                    pool.wait_ge(s_stA, g - 1)
                for j in range(GT):
                    pool.indirect_dma_start(ymlp[g % 2][:, j * D:(j + 1) * D], None, mlp_rows,
                                            bass.IndirectOffsetOnAxis(ap=slot[:, g * GT + j:g * GT + j + 1], axis=0),
                                            bounds_check=ST * P - 1, oob_is_err=False
                                            ).then_inc(s_yback[g % 2], 16)

            def attention(l):
                def step(i):
                    if l == 0 and 0 <= i - 2 < G:
                        mlp_norm(i)
                    if 0 <= i < G:
                        norm_probs(l, i)
                    if i <= G and (l, i) != (0, -2):
                        rsqrt(l, i)
                    if l == 1 and i + 4 < G and i >= -2:
                        gather_back(i + 4)
                each_step(l, step)

            def route(l):
                def low_part(e):
                    pool.wait_ge(s_whi, l * E + e + 1)
                    part = slice(e * F, (e + 1) * F)
                    pool.tensor_tensor(W1_lo[l][:, part], W1[l][:, part], W1_hi[:, part].bitcast(F32), ALU.subtract
                                       ).then_inc(s_wlo, 1)

                for e in range(E - 2):
                    low_part(e)
                for k in range(TILES // HT):
                    pool.wait_ge(s_eqhi, l * TILES // HT + k + 1)
                    if l == 1:
                        pool.wait_ge(s_invm, TILES)
                    pool.tensor_tensor(in_hi[k][:, 0, :, :], eq_hi[k], tile1[:, k * HT:(k + 1) * HT].unsqueeze(2
                                       ).to_broadcast([P, HT, ST]), ALU.mult).then_inc(s_inhi, 1)
                for e in range(E - 2, E):
                    low_part(e)

            def gather(l, s):
                if s >= 6:
                    pool.wait_ge(s_rt if l == 0 else s_yb, l * ST + s - 5)
                pool.indirect_dma_start(rows[s % 6][:, 0:(D, RW)[l]], None, tok_rows[l],
                                        bass.IndirectOffsetOnAxis(ap=src[:, s:s + 1], axis=0),
                                        bounds_check=TOK - 1, oob_is_err=False).then_inc(s_row_in[l][s % 6], 16)

            def scatter(s):
                pool.wait_ge(s_yb, ST + s + 1)
                pool.indirect_dma_start(out_rows, bass.IndirectOffsetOnAxis(ap=dst[:, s:s + 1], axis=0),
                                        ob[s % 3][:, :], None,
                                        bounds_check=TOK - 1, oob_is_err=False).then_inc(s_scat[s % 3], 16)

            for l in range(2):
                attention(l)
                route(l)
                pool.wait_ge(s_src, l + 1)
                for h in range(3):
                    pool.wait_ge(s_store[h], stored_rows(l, h))
                for s in range(ST + 6 * l):
                    if s < ST:
                        gather(l, s)
                    if l == 1 and s >= 6:
                        scatter(s - 6)
                if l == 0:
                    pool.wait_ge(s_h, ST)
                    pool.memset(prT[0], 0.0).then_inc(s_zero, 1)
                    pool.memset(prT[1], 0.0).then_inc(s_zero, 1)
                    for r in range(3):
                        pool.wait_ge(s_out[r], 16 * (ST // 3))
                    gather_back(0)
                    gather_back(1)

        @block.scalar
        def _(act):
            act.dma_start(WT[0][0][:, :], t["L0_xattn_Wq"]).then_inc(s_wload[0], 16)
            act.dma_start(WT[0][1][:, :], t["L0_xattn_Wk"]).then_inc(s_wload[0], 16)
            act.dma_start(WT[0][2][:, :], t["L0_xattn_Wv"]).then_inc(s_wload[0], 16)
            for m in range(3):
                act.dma_start(WT[1][m][:, :], t[f"L1_xattn_W{'qkv'[m]}"]).then_inc(s_wload[0], 16)
            for l in range(2):
                act.wait_ge(s_wt, l + 1)
                for m in range(3):
                    ins = act.copy(WT[l][m][:, :], bank[6 + l][:, m * D:(m + 1) * D])
                ins.then_inc(s_wtc, 1)
            act.wait_ge(s_bias, 16 * 8)
            act.activation(tanh_g[:, :], graw[:, :], ACT.Tanh).then_inc(s_tanh, 1)

            def route(l):
                act.wait_ge(s_pv, n(l, G - 1))
                act.wait_ge(s_lg, n(l, G - 1))
                if l == 0:
                    act.wait_ge(s_wtc, 2 + 2 * E)
                else:
                    act.wait_ge(s_l1w, 32)
                for e in range(E):
                    part = slice(e * F, (e + 1) * F)
                    act.copy(W1_hi[:, part], W1[l][:, part]).then_inc(s_whi, 1)
                for k in range(TILES // HT):
                    act.wait_ge(s_eqhi, l * TILES // HT + k + 1)
                    act.activation(in_hi[k][:, 1, :, :], eq_hi[k], ACT.Copy, scale=own_p[:, 0:1]).then_inc(s_inhi_p, 1)

            def copy_weights(part):
                for k in range(part * E // 2, (part + 1) * E // 2):
                    act.wait_ge(s_wt, 2 + k + 1)
                    to = W1[0] if k < E else W2[0]
                    act.copy(to[:, (k % E) * F:(k % E + 1) * F], (pK, pQ)[k % 2][:, :]).then_inc(s_wtc, 1)

            def attention(l):
                def step(i):
                    a, b, c, z = i - 1, i + 1, i + 2, i - 2
                    if 0 <= a < G:
                        act.wait_ge(s_pT, n(l, a))
                        wait_group(act, s_pv, l, a - 2)
                        if n(l, a) <= 2:
                            act.wait_ge(s_const, N_CONST)
                        if l == 1 and a < 2:
                            act.wait_ge(s_zero, 2)
                        pP3 = pP[0:S, :].rearrange("p (j c) -> p j c", j=GT)
                        for h in range(2):
                            part = slice(h * S, (h + 1) * S)
                            ins = act.copy(prT[a % 2][part, :, part], pP3[:, :, part])
                        ins.then_inc(s_pTc, 1)
                    if 0 <= b < G:
                        act.wait_ge(s_nm, n(l, b))
                        wait_group(act, s_xT, l, b - 2)
                        for j in range(GT):
                            ins = act.activation(xn[b % 2][:, j, :], X[:, b * W + j * D:b * W + (j + 1) * D],
                                                 ACT.Identity, bias=nmA[i % 2][:, j:j + 1],
                                                 scale=pout[(i - 1) % 2][:, j:j + 1])
                        ins.then_inc(s_xn, 1)
                    if 0 <= i < G:
                        act.wait_ge(s_max, n(l, i))
                        wait_group(act, s_prn, l, i - 2)
                        for j in range(GT):
                            ins = act.activation(pr[i % 2][:, j, :], pS[:, j * S:(j + 1) * S], ACT.Exp,
                                                 bias=nmx[:, j:j + 1], scale=D ** -0.5 if l == 0 else 1.0,
                                                 accum_out=den[i % 2][:, j:j + 1])
                        ins.then_inc(s_exp, 1)
                    if l == 1 and 0 <= i - 3:
                        act.wait_ge(s_gsub, i - 2)
                        act.activation(gs[:, :, :], gl[:, :, :], ACT.Exp).then_inc(s_gexp, 1)
                    if 0 <= b < G:
                        act.wait_ge(s_xT, n(l, b))
                        wait_group(act, s_q, l, b - 2)
                        act.copy(xnT[b % 2][:, :], pT[:, :]).then_inc(s_xTc, 1)
                    if 0 <= b < G:
                        act.wait_ge(s_k, n(l, b))
                        act.activation(kT[b % 2][:, :], pK[:, :], ACT.Identity,
                                       bias=bias_qk[:, 2 * l + 1:2 * l + 2]).then_inc(s_kc, 1)
                    if 0 <= z < G:
                        act.wait_ge(s_nmB, n(l, z))
                        waits_stored(act, l, z)
                        if l == 1:
                            wait_group(act, s_x2T, 1, z - 3)
                        scales = 2 * GT if l == 0 else GT
                        for j in range(GT - 1 if l == 0 else GT // 2, GT):
                            ins = act.activation(hat[z % 3][:, j, 0:D], X[:, z * W + j * D:z * W + (j + 1) * D],
                                                 ACT.Identity, bias=nmB[i % 2][:, j:j + 1],
                                                 scale=pout[(i - 1) % 2][:, scales + j:scales + j + 1])
                        ins.then_inc(s_hat, 1)
                    if 0 <= z < G and l == 0:
                        act.wait_ge(s_x2T, n(l, z))
                        wait_group(act, s_lg, l, z - 2)
                        act.copy(xn2T[z % 2][:, :], pC[:, :]).then_inc(s_x2Tc, 1)
                    if 0 <= b < G:
                        act.wait_ge(s_q, n(l, b))
                        act.activation(qT[b % 2][:, :], pQ[:, :], ACT.Identity,
                                       bias=bias_qk[:, 2 * l:2 * l + 1]).then_inc(s_qc, 1)
                    if 0 <= z < G and l == 1:
                        act.wait_ge(s_x2T, n(l, z))
                        wait_group(act, s_lg, l, z - 2)
                        act.copy(xn2T[z % 2][:, :], pC[:, :]).then_inc(s_x2Tc, 1)
                    if 0 <= c < G and l == 0:
                        act.wait_ge(s_cT, c + 1)
                        act.copy(ctxT[:, cols(c)], pC[:, :]).then_inc(s_cTc, 1)
                    if l == 0 and i >= G - 1:
                        copy_weights(i - (G - 1))
                each_step(l, step)

            def mlp(l):
                func = ACT.Relu if l == 0 else ACT.Gelu

                def step(q, r, expert):
                    q2, r2 = ahead(q, r, 2)
                    if valid(q2, r2):
                        if l == 0:
                            act.wait_ge(s_rtc, num(q2, r2) + 1)
                        else:
                            act.wait_ge(s_rt, ST + num(q2, r2) + 1)
                        if has_before(l, q2, r2, 3):
                            act.wait_ge(s_h, l * ST + num(q2, r2) - 2)
                        act.copy(rT_hi[r2 % 3][:, :], rT[r2 % 3][:, :] if l == 0 else pX[:, 0:P]).then_inc(s_rhi, 1)
                    if valid(q, r):
                        act.wait_ge(s_ht, l * ST + num(q, r) + 1)
                        if has_before(l, q, r, 3):
                            act.wait_ge(s_y, l * ST + num(q, r) - 2)
                        act.activation(hT[r % 3][:, :], pHT[r % 3][:, :], func).then_inc(s_hTc, 1)
                each_tile(act, 2, 0, step)

            attention(0)
            act.wait_ge(s_azs, 1)
            act.activation(alpha[:, :], top[:, :], ACT.Exp, scale=-1.0).then_inc(s_aexp, 1)
            route(0)
            mlp(0)
            attention(1)
            route(1)
            mlp(1)

        @block.vector
        def _(dve):
            chain = [0]

            def link(ins):
                chain[0] += 1
                ins.then_inc(s_dve, 1)
                dve.wait_ge(s_dve, chain[0])

            def mark(ins):
                chain[0] += 1
                ins.then_inc(s_dve, 1)
                return chain[0]

            dve.memset(pin[0][:, :], 1.0)
            link(dve.memset(pin[1][:, :], 1.0))

            def gate_norms():
                dve.wait_ge(s_small, 16 * 5)
                link(dve.tensor_tensor(wg_sq[:, :], wg_raw[:, :], wg_raw[:, :], ALU.mult))
                link(dve.reduce_sum(wg_ss[:, :], wg_sq[:, :], X_AXIS))
                dve.tensor_scalar(wg_ss[:, :], wg_ss[:, :], GATE_EPS ** 2, None, ALU.max).then_inc(s_gate, 1)

            def gate_unit():
                dve.wait_ge(s_gate, 2)
                dve.tensor_scalar(wg_u[:, :], wg_raw[:, :], wg_r[:, :], None, ALU.mult).then_inc(s_gate, 1)

            def gate_weights():
                dve.wait_ge(s_gate, 4)
                dve.tensor_copy(gateT[0][:, :], bank[7][:, 0:E])
                dve.tensor_copy(ln_gT[:, :], bank[7][:, E:2 * E])
                dve.tensor_copy(ln_bT[:, :], bank[7][:, 2 * E:3 * E])
                dve.tensor_copy(wg_uT[:, :], bank[7][0:R, 3 * E:4 * E]).then_inc(s_gate, 1)

            def gate_product():
                dve.wait_ge(s_gate, 6)
                dve.tensor_copy(gateT[1][:, :], bank[7][:, 4 * E:5 * E]).then_inc(s_gate, 1)

            def bn(g):
                for j in range(GT):
                    ins = dve.bn_stats(bn6[:, j, :], X[:, g * W + j * D:g * W + (j + 1) * D])
                return mark(ins)

            def aggregate(g, mv):
                for j in range(GT):
                    ins = dve.bn_aggr(mv[g % 2][:, j, :], bn6[:, j, :])
                return mark(ins)

            def attention(l):
                scale = D ** -0.5 if l == 0 else 1.0

                def step(i):
                    a, c, y, z = i - 1, i + 2, i - 3, i - 2
                    if (l, i) == (0, 1):
                        gate_weights()

                    def mlp_norms():
                        if l == 0:
                            wait_group(dve, s_x2T, l, z - 2)
                            for j in range(GT):
                                ins = dve.tensor_scalar(xn2[z % 2][:, j, :], X[:, z * W + j * D:z * W + (j + 1) * D],
                                                        mvB[z % 2][:, j, 0:1], po[:, GT + j:GT + j + 1],
                                                        ALU.subtract, ALU.mult)
                            ins.then_inc(s_xn2, 1)
                        else:
                            waits_stored(dve, 1, z)
                            wait_group(dve, s_x2T, 1, z - 3)
                            for j in range(GT // 2):
                                ins = dve.tensor_scalar(hat[z % 3][:, j, 0:D], X[:, z * W + j * D:z * W + (j + 1) * D],
                                                        mvB[z % 2][:, j, 0:1], po[:, GT + j:GT + j + 1],
                                                        ALU.subtract, ALU.mult)
                            ins.then_inc(s_xn2, 1)

                    if 0 <= c < G and l == 0:
                        dve.wait_ge(s_in[c % 2], 32 * (c // 2 + 1))
                        taken = bn(c)
                    if 0 <= c < G and l == 1:
                        dve.wait_ge(s_yback[c % 2], 16 * GT * (c // 2 + 1))
                        for j in range(GT):
                            xs = X[:, c * W + j * D:c * W + (j + 1) * D]
                            ins = dve.scalar_tensor_tensor(xs, ymlp[c % 2][:, j * D:(j + 1) * D],
                                                           alpha[:, c * GT + j:c * GT + j + 1], xs,
                                                           ALU.mult, ALU.add)
                        ins.then_inc(s_stA, 1)
                    if i >= -1 and i - 1 <= G:
                        dve.wait_ge(s_pow, l * POWS + i - 1 + 3)
                    po = pout[(i - 1) % 2]
                    if 0 <= i + 1 < G:
                        b = i + 1
                        wait_group(dve, s_xn, l, b - 2)
                        dve.scalar_tensor_tensor(nmA[i % 2][:, :], mvA[b % 2][:, :, 0], -1.0, po[:, 0:GT],
                                                 ALU.mult, ALU.mult).then_inc(s_nm, 1)
                    if 0 <= z < G:
                        wait_group(dve, s_hat, l, z - 2)
                        dve.scalar_tensor_tensor(nmB[i % 2][:, :], mvB[z % 2][:, :, 0], -1.0,
                                                 po[:, 2 * GT:3 * GT] if l == 0 else po[:, GT:2 * GT],
                                                 ALU.mult, ALU.mult).then_inc(s_nmB, 1)
                    if 0 <= c < G and l == 0:
                        dve.wait_ge(s_dve, taken)
                        taken = aggregate(c, mvA)
                    if z == G - 1:
                        mlp_norms()
                    if 0 <= c < G and l == 1:
                        dve.wait_ge(s_stA, c + 1)
                        taken = bn(c)
                    if 0 <= y:
                        dve.wait_ge(s_lg, n(l, y))
                        lg = LG[:, y * GT:(y + 1) * GT, :]
                        dve.tensor_copy(lg, pL.rearrange("p (j e) -> p j e", j=GT)).then_inc(s_lgc, 1)
                    if 0 <= i < G:
                        dve.wait_ge(s_sc, n(l, i))
                        if 0 <= y:
                            dve.wait_ge(s_lg, n(l, y))
                        ps = pS[:, 0:GT * S].rearrange("p (j c) -> p j c", j=GT)
                        maxima = mark(dve.reduce_max(mx[:, :], ps, X_AXIS))
                    if l == 1 and 0 <= y:
                        dve.wait_ge(s_lgc, n(1, y))
                        gate_max = mark(dve.reduce_max(gm[:, :], lg, X_AXIS))
                    if 0 <= i < G:
                        dve.wait_ge(s_dve, maxima)
                        dve.tensor_scalar(nmx[:, :], mx[:, :], -scale, None, ALU.mult).then_inc(s_max, 1)
                    if l == 1 and 0 <= y:
                        dve.wait_ge(s_dve, gate_max)
                        dve.tensor_tensor(gl[:, :, :], lg, gm[:, :].unsqueeze(2).to_broadcast([P, GT, E]),
                                          ALU.subtract).then_inc(s_gsub, 1)
                    if 0 <= c < G:
                        dve.wait_ge(s_dve, taken)
                        if l == 1:
                            dve.wait_ge(s_dve, aggregate(c, mvA))
                        asked = mark(dve.tensor_scalar(pin[i % 2][:, 0:GT], mvA[c % 2][:, :, 1], EPS, None, ALU.add))
                    if (l, i) == (0, 1):
                        gate_product()
                    if 0 <= z < G - 1 and l == 0:
                        mlp_norms()
                    if 0 <= a < G:
                        dve.wait_ge(s_pv, n(l, a))
                        dve.tensor_tensor(X[:, cols(a)], X[:, cols(a)], pO[:, :], ALU.add).then_inc(s_x1, 1)
                        dve.wait_ge(s_x1, n(l, a))
                        taken = bn(a)
                    if 0 <= i < G:
                        dve.wait_ge(s_exp, n(l, i))
                        reciprocals = mark(dve.reciprocal(rden[:, :], den[i % 2][:, :]))
                    if 0 <= a < G:
                        dve.wait_ge(s_dve, taken)
                        taken = aggregate(a, mvB)
                    if 0 <= i < G:
                        wait_group(dve, s_prn, l, i - 2)
                        if n(l, i) == 1:
                            dve.wait_ge(s_tanh, 1)
                        dve.wait_ge(s_dve, reciprocals)
                        dve.tensor_scalar(rdg[i % 2][:, :], rden[:, :], tanh_g[:, l:l + 1], None, ALU.mult
                                          ).then_inc(s_rd, 1)
                    if 0 <= a < G:
                        dve.wait_ge(s_dve, taken)
                        dve.tensor_scalar(pin[i % 2][:, GT:2 * GT], mvB[a % 2][:, :, 1], EPS, None, ALU.add)
                        asked = mark(dve.tensor_scalar(pin[i % 2][:, 2 * GT:3 * GT], mvB[a % 2][:, :, 1], 1.0 + EPS,
                                                       EPS * EPS, ALU.mult, ALU.add))
                    if i <= G:
                        dve.wait_ge(s_dve, asked)
                        dve.engine_nop().then_inc(s_pin, 1)
                    if 0 <= z < G - 1 and l == 1:
                        mlp_norms()
                    if 0 <= i < G:
                        dve.wait_ge(s_v, n(l, i))
                        wait_group(dve, s_pv, l, i - 2)
                        if n(l, i) == 1:
                            dve.wait_ge(s_bias, 16 * 8)
                        dve.tensor_tensor(v[i % 2][:, :, :], tiles3(pV[:, :]),
                                          bias_v[:, l:l + 1, :].to_broadcast([P, GT, D]), ALU.add
                                          ).then_inc(s_vc, 1)
                    if 0 <= z < G and l == 0:
                        dve.wait_ge(s_xn2, z + 1)
                        dve.wait_ge(s_hat, z + 1)
                        dve.wait_ge(s_hat_pool, z + 1)
                        dve.scalar_tensor_tensor(tiles3(X[:, cols(z)]), xn2[z % 2][:, :, :], tanh_g[:, 2:3],
                                                 tiles3(X[:, cols(z)]), ALU.mult, ALU.add).then_inc(s_x2, 1)
                    if (l, i) == (0, -1):
                        gate_norms()
                    if (l, i) == (0, 0):
                        gate_unit()
                    if l == 1 and 0 <= y:
                        dve.wait_ge(s_gexp, y + 1)
                        link(dve.reduce_sum(gd[:, :], gs[:, :, :], X_AXIS))
                        link(dve.reciprocal(gm[:, :], gd[:, :]))
                        dve.tensor_scalar(hat[y % 3][:, :, D], gm[:, :], tanh_g[:, 3:4], None, ALU.mult
                                          ).then_inc(s_score, 1)
                each_step(l, step)
                if l == 0:
                    dve.wait_ge(s_const, N_CONST)

            def route(l):
                dve.wait_ge(s_lgc, n(l, G - 1))
                ins = dve.reduce_max(top[:, :], LG[:, :, :], X_AXIS)
                if l == 0:
                    ins.then_inc(s_azs, 1)
                    dve.wait_ge(s_azs, 1)
                else:
                    link(ins)
                te = [P, TILES, E]
                link(dve.tensor_tensor(hit[:, :, :], LG[:, :, :], top[:, :].unsqueeze(2).to_broadcast(te), ALU.is_equal))
                link(dve.tensor_tensor(hit[:, :, :], hit[:, :, :], iota_e[:, :].unsqueeze(1).to_broadcast(te), ALU.mult))
                link(dve.tensor_reduce(first[:, :], hit[:, :, :], X_AXIS, ALU.min))
                link(dve.tensor_tensor(oh[:, :, :].rearrange("p e t -> p t e"), first[:, :].unsqueeze(2).to_broadcast(te),
                                       iota_e[:, :].unsqueeze(1).to_broadcast(te), ALU.is_equal))
                dve.reduce_sum(cnt[:, :], oh[:, :, :], X_AXIS).then_inc(s_cnt, 1)
                link(dve.tensor_tensor_scan(cum[:, :, :].rearrange("p e t -> p (e t)"), ones_et[:, :],
                                            oh[:, :, :].rearrange("p e t -> p (e t)"), 0.0, ALU.mult, ALU.add))
                link(dve.tensor_tensor(ends[:, :], cum[:, :, TILES - 1], cnt[:, :], ALU.subtract))
                link(dve.tensor_scalar(ends[:, :], ends[:, :], 1.0, None, ALU.add))
                dve.wait_ge(s_pfx, l + 1)
                link(dve.tensor_scalar(tf[:, :], bank[0][:, E:2 * E], float(P - 1), None, ALU.add))
                link(dve.tensor_copy(ti[:, :], tf[:, :]))
                link(dve.tensor_scalar(ti[:, :], ti[:, :], 7, None, ALU.logical_shift_right))
                link(dve.tensor_copy(tcnt[:, :], ti[:, :]))
                link(dve.tensor_tensor_scan(tend[:, :], ones_et[:, 0:E], tcnt[:, :], 0.0, ALU.mult, ALU.add))
                link(dve.tensor_tensor(off[:, :], tend[:, :], tcnt[:, :], ALU.subtract))
                link(dve.scalar_tensor_tensor(off[:, :], off[:, :], float(P), bank[0][:, 0:E], ALU.mult, ALU.add))
                link(dve.tensor_tensor(off[:, :], off[:, :], ends[:, :], ALU.subtract))
                et = [P, E, TILES]
                link(dve.tensor_tensor(cum[:, :, :], cum[:, :, :], off[:, :].unsqueeze(2).to_broadcast(et), ALU.add))
                link(dve.tensor_tensor(cum[:, :, :], cum[:, :, :], oh[:, :, :], ALU.mult))
                link(dve.reduce_sum(slot_f[:, :], cum[:, :, :].rearrange("p e t -> p t e"), X_AXIS))
                link(dve.tensor_copy(slot[:, :], slot_f[:, :]))
                dve.tensor_scalar(hi_i[:, :], slot[:, :], 7, None, ALU.logical_shift_right)
                link(dve.tensor_scalar(lo_i[:, :], slot[:, :], P - 1, None, ALU.bitwise_and))
                dve.tensor_copy(hi[:, :], hi_i[:, :])
                dve.tensor_copy(lo[:, :], lo_i[:, :]).then_inc(s_hilo, 1)
                dve.wait_ge(s_hilo, l + 1)
                for g in range(G):
                    if g % 2 == 0:
                        wide = [P, HT, ST]
                        dve.tensor_tensor(eq_hi[g // 2], iota_s[:, :].unsqueeze(1).to_broadcast(wide),
                                          hi[:, g * GT:g * GT + HT].unsqueeze(2).to_broadcast(wide), ALU.is_equal
                                          ).then_inc(s_eqhi, 1)
                    cols4 = slice(g * GT, (g + 1) * GT)
                    dve.tensor_tensor(in_lo[g][:, :, :], iota_p[:, :].unsqueeze(1).to_broadcast([P, GT, P]),
                                      lo[:, cols4].unsqueeze(2).to_broadcast([P, GT, P]), ALU.is_equal
                                      ).then_inc(s_lo, 1)
                dve.wait_ge(s_invm, (l + 1) * TILES)
                link(dve.tensor_copy(inv_f[:, :], pV[:, 0:2 * ST]))
                link(dve.scalar_tensor_tensor(src_f[:, :], inv_f[:, 0:ST], float(P), inv_f[:, ST:2 * ST],
                                              ALU.mult, ALU.add))
                link(dve.tensor_scalar(src_f[:, :], src_f[:, :], -float(P), 0.0, ALU.add, ALU.max))
                if l == 1:
                    link(dve.tensor_scalar(dst_f[:, :], inv_f[:, 0:ST], 0.0, EMPTY, ALU.is_equal, ALU.mult))
                    link(dve.tensor_tensor(dst_f[:, :], dst_f[:, :], src_f[:, :], ALU.add))
                    link(dve.tensor_copy(dst[:, :], dst_f[:, :]))
                dve.tensor_copy(src[:, :], src_f[:, :]).then_inc(s_src, 1)
                we = [1, TURNS * WIN, E]
                link(dve.tensor_tensor(ge[:, :, :], iota_w[0:1, :, :].rearrange("p q k -> p (q k)").unsqueeze(2).to_broadcast(we),
                                       tend[0:1, :].unsqueeze(1).to_broadcast(we), ALU.is_ge))
                link(dve.reduce_sum(eid_f[:, :], ge[:, :, :], X_AXIS))
                link(dve.tensor_scalar(eid_f[:, :], eid_f[:, :], float(E - 1), None, ALU.min))
                dve.tensor_copy(eid[:, :], eid_f[:, :]).then_inc(s_eid, 1)
                if l == 0:
                    dve.wait_ge(s_aexp, 1)
                    link(dve.tensor_scalar(alpha[:, :], alpha[:, :], 1.0, None, ALU.add))
                    link(dve.reciprocal(alpha[:, :], alpha[:, :]))
                    link(dve.tensor_scalar(alpha[:, :], alpha[:, :], tanh_g[:, 2:3], None, ALU.mult))

            def mlp(l):
                base = l * ST
                dve.wait_ge(s_eid, l + 1)
                dve.wait_ge(s_wload[3], 48 + 16 * l)

                def low_part(q2, r2):
                    dve.wait_ge(s_rhi, base + num(q2, r2) + 1)
                    if has_before(l, q2, r2, 3):
                        dve.wait_ge(s_h, base + num(q2, r2) - 2)
                    dve.tensor_tensor(rT_lo[r2 % 3][:, :], rT[r2 % 3][:, :] if l == 0 else pX[:, 0:P],
                                      rT_hi[r2 % 3][:, :].bitcast(F32), ALU.subtract).then_inc(s_rlo, 1)

                def step(q, r, expert):
                    q2, r2 = ahead(q, r, 2)
                    q1, r1 = ahead(q, r, 1)
                    q0, rp = ahead(q, r, -1)
                    if l == 0 and valid(q2, r2):
                        ev = expert(2)
                        dve.wait_ge(s_rt, num(q2, r2) + 1)
                        if has_before(0, q2, r2, 3):
                            dve.wait_ge(s_rlo, num(q2, r2) - 2)
                        dve.tensor_scalar(rT[r2 % 3][:, :], pX[:, 0:P], ln_gT[:, bass.ds(ev, 1)],
                                          ln_bT[:, bass.ds(ev, 1)], ALU.mult, ALU.add).then_inc(s_rtc, 1)
                    if valid(q2, r2) and l == 1:
                        low_part(q2, r2)
                    if valid(q1, r1):
                        ev = expert(1)
                        dve.wait_ge(s_h, base + num(q1, r1) + 1)
                        if has_before(l, q1, r1, 3):
                            dve.wait_ge(s_ht, base + num(q1, r1) - 2)
                        dve.tensor_tensor(hb[r1 % 3][:, :], pH[r1 % 3][:, :], B1[:, bass.ds(ev * F, F)], ALU.add
                                          ).then_inc(s_hb, 1)
                    if valid(q2, r2) and l == 0:
                        low_part(q2, r2)
                    if valid(q0, rp):
                        ev = expert(-1)
                        dve.wait_ge(s_y, base + num(q0, rp) + 1)
                        if l == 0:
                            if has_before(0, q0, rp, 3):
                                dve.wait_ge(s_out[rp % 3], 16 * third(q0, rp))
                            dve.tensor_tensor(yb[rp % 3][:, :], pY[:, 0:D], B2[l][:, bass.ds(ev * D, D)], ALU.add
                                              ).then_inc(s_yb, 1)
                        else:
                            if has_before(0, q0, rp, 3):
                                dve.wait_ge(s_scat[rp % 3], 16 * third(q0, rp))
                            link_y(dve.tensor_tensor(yb[rp % 3][:, :], pY[:, 0:D], B2[l][:, bass.ds(ev * D, D)], ALU.add),
                                   num(q0, rp) + 1)
                            dve.scalar_tensor_tensor(ob[rp % 3][:, :], yb[rp % 3][:, :], rows[rp % 6][:, D:D + 1],
                                                     rows[rp % 6][:, D + 4:RW], ALU.mult, ALU.add).then_inc(s_yb, 1)

                def link_y(ins, value):
                    ins.then_inc(s_y1, 1)
                    dve.wait_ge(s_y1, value)
                each_tile(dve, 2, 1, step, with_experts=True)

            attention(0)
            route(0)
            mlp(0)
            attention(1)
            route(1)
            mlp(1)

        @block.tensor
        def _(pe):
            def tile_of(ap, j, w=D):
                return ap[:, j * w:(j + 1) * w]

            def transpose_ctx(g):
                pe.wait_ge(s_in[g % 2], 32 * (g // 2 + 1))
                if g >= 1:
                    pe.wait_ge(s_cTc, g)
                for j in range(GT):
                    ins = pe.transpose(tile_of(pC, j), ctx_raw[g % 2][:, j, :], ident[:, :])
                ins.then_inc(s_cT, 1)

            pe.wait_ge(s_ident, 2)
            pe.wait_ge(s_wload[0], 96)
            for l in range(2):
                for m in range(3):
                    ins = pe.transpose(bank[6 + l][:, m * D:(m + 1) * D], WT[l][m][:, :], ident[:, :])
                ins.then_inc(s_wt, 1)

            def gate_weights():
                pe.wait_ge(s_small, 16 * 5)
                pe.wait_ge(s_gate, 3)
                for m in range(3):
                    pe.transpose(bank[7][:, m * E:(m + 1) * E], raw_small[:, m, :], ident[0:E, 0:E])
                pe.transpose(bank[7][0:R, 3 * E:4 * E], wg_u[:, :], ident[0:E, 0:E]).then_inc(s_gate, 1)

            def gate_product():
                pe.wait_ge(s_gate, 5)
                pe.matmul(bank[7][:, 4 * E:5 * E], wg_red[:, :], wg_uT[:, :], start=True, stop=True).then_inc(s_gate, 1)

            def transpose_weights(part):
                if part == 0:
                    pe.wait_ge(s_wload[1], 16)
                    pe.wait_ge(s_wload[2], 16)
                    pe.wait_ge(s_kc, G)
                    pe.wait_ge(s_qc, G)
                for k in range(part * E // 2, (part + 1) * E // 2):
                    if k >= 2:
                        pe.wait_ge(s_wtc, 2 + k - 1)
                    raw = W1[1] if k < E else W2[1]
                    for c in range(FC):
                        col = (k % E) * F + c * P
                        ins = pe.transpose((pK, pQ)[k % 2][:, c * P:(c + 1) * P], raw[:, col:col + P], ident[:, :])
                    ins.then_inc(s_wt, 1)

            def attention(l):
                wq, wk, wv = (w[:, :] for w in WT[l])

                def step(i):
                    a, b, c, y, z = i - 1, i + 1, i + 2, i - 3, i - 2
                    if 0 <= a < G:
                        pe.wait_ge(s_prn, n(l, a))
                        wait_group(pe, s_pTc, l, a - 1)
                        for j in range(GT):
                            ins = pe.transpose(pP[0:S, j * P:(j + 1) * P], prn[a % 2][:, j, :], ident[:, :])
                        ins.then_inc(s_pT, 1)
                    if 0 <= i < G:
                        pe.wait_ge(s_kc, n(l, i))
                        pe.wait_ge(s_qc, n(l, i))
                        wait_group(pe, s_exp, l, i - 1)
                        wait_group(pe, s_lgc, l, y - 1)
                        for j in range(GT):
                            for h in range(2):
                                at = j * P + h * S
                                ins = pe.matmul(pS[h * S:(h + 1) * S, j * S:(j + 1) * S], qT[i % 2][:, at:at + S],
                                                kT[i % 2][:, at:at + S], start=True, stop=True)
                        ins.then_inc(s_sc, 1)
                    if 0 <= y:
                        pe.wait_ge(s_x2Tc, n(l, y))
                        wait_group(pe, s_lgc, l, y - 1)
                        for j in range(GT):
                            ins = pe.matmul(tile_of(pL, j, E), tile_of(xn2T[y % 2], j), gateT[l][:, :],
                                            start=True, stop=True)
                        ins.then_inc(s_lg, 1)
                    if 0 <= b < G:
                        if l == 0:
                            pe.wait_ge(s_cTc, b + 1)
                        if n(l, b) == 1:
                            pe.wait_ge(s_wtc, 2)
                        wait_group(pe, s_kc, l, b - 1)
                        pe.matmul(pK[:, :], wk, ctxT[:, cols(b)], start=True, stop=True).then_inc(s_k, 1)
                    if (l, i) == (0, 1):
                        gate_product()
                    if 0 <= a < G:
                        pe.wait_ge(s_pTc, n(l, a))
                        pe.wait_ge(s_vc, n(l, a))
                        wait_group(pe, s_x1, l, a - 1)
                        if (l, a) == (0, 0):
                            pe.wait_ge(s_gate, 7)
                        for j in range(GT):
                            ins = pe.matmul(tile_of(pO, j), prT[a % 2][:, j, :], v[a % 2][:, j, :],
                                            start=True, stop=True)
                        ins.then_inc(s_pv, 1)
                    if 0 <= b < G:
                        pe.wait_ge(s_xn, n(l, b))
                        wait_group(pe, s_xTc, l, b - 1)
                        for j in range(GT):
                            ins = pe.transpose(tile_of(pT, j), xn[b % 2][:, j, :], ident[:, :])
                        ins.then_inc(s_xT, 1)
                    if 0 <= z < G and l == 0:
                        pe.wait_ge(s_xn2, n(0, z))
                        pe.wait_ge(s_cTc, min(c, G))
                        for j in range(GT):
                            ins = pe.transpose(tile_of(pC, j), xn2[z % 2][:, j, 0:D], ident[:, :])
                        ins.then_inc(s_x2T, 1)
                    if 0 <= i < G:
                        wait_group(pe, s_vc, l, i - 1)
                        for j in range(GT):
                            ins = pe.matmul(tile_of(pV, j), tile_of(ctxT[:, cols(i)], j), wv, start=True, stop=True)
                        ins.then_inc(s_v, 1)
                    if 0 <= b < G:
                        pe.wait_ge(s_xTc, n(l, b))
                        wait_group(pe, s_qc, l, b - 1)
                        pe.matmul(pQ[:, :], wq, xnT[b % 2][:, :], start=True, stop=True).then_inc(s_q, 1)
                    if 0 <= z < G and l == 1:
                        pe.wait_ge(s_xn2, n(1, z))
                        pe.wait_ge(s_hat, n(1, z))
                        wait_group(pe, s_x2Tc, 1, z - 1)
                        for j in range(GT):
                            ins = pe.transpose(tile_of(pC, j), hat[z % 3][:, j, 0:D], ident[:, :])
                        ins.then_inc(s_x2T, 1)
                    if 0 <= c < G and l == 0:
                        if z >= 0:
                            pe.wait_ge(s_x2Tc, z + 1)
                        transpose_ctx(c)
                    if l == 0 and i >= G - 1:
                        transpose_weights(i - (G - 1))
                    if (l, i) == (0, 0):
                        gate_weights()
                each_step(l, step)

            def route(l):
                pe.wait_ge(s_cnt, l + 1)
                pe.matmul(bank[0][:, 0:E], before[:, :], cnt[:, :], start=True, stop=True)
                pe.matmul(bank[0][:, E:2 * E], ones[:, :], cnt[:, :], start=True, stop=True).then_inc(s_pfx, 1)
                for tt in range(TILES):
                    if tt % GT == 0:
                        pe.wait_ge(s_lo, l * G + tt // GT + 1)
                    if tt % HT == 0:
                        pe.wait_ge(s_inhi, l * TILES // HT + tt // HT + 1)
                        pe.wait_ge(s_inhi_p, l * TILES // HT + tt // HT + 1)
                    pe.matmul(pV[:, 0:2 * ST], in_lo[tt // GT][:, tt % GT, :], in_hi[tt // HT][:, :, tt % HT, :],
                              start=(tt == 0), stop=(tt == TILES - 1)).then_inc(s_invm, 1)
                if l == 0:
                    pe.wait_ge(s_wtc, 2 + 2 * E)
                else:
                    pe.wait_ge(s_l1w, 32)

            def mlp(l):
                base = l * ST
                pe.wait_ge(s_eid, l + 1)
                pe.wait_ge(s_src, l + 1)
                pe.wait_ge(s_wlo, (l + 1) * E)

                def step(q, r, expert):
                    q2, r2 = ahead(q, r, 2)
                    q1, r1 = ahead(q, r, 1)
                    q0, rp = ahead(q, r, -1)
                    if valid(q2, r2):
                        pe.wait_ge(s_row_in[l][r2 % 6], 16 * (U // 6 * q2 + r2 // 6 + 1))
                        if has_before(l, q2, r2, 1):
                            pe.wait_ge(s_rtc if l == 0 else s_rlo, base + num(q2, r2))
                        pe.transpose(pX[:, 0:P], rows[r2 % 6][:, 0:D], ident[:, :]).then_inc(s_rt, 1)
                    if valid(q1, r1):
                        ev = expert(1)
                        pe.wait_ge(s_rlo, base + num(q1, r1) + 1)
                        if has_before(l, q1, r1, 3):
                            pe.wait_ge(s_hb, base + num(q1, r1) - 2)
                        pe.matmul(pH[r1 % 3][:, :], rT_hi[r1 % 3][:, :], W1_hi[:, bass.ds(ev * F, F)],
                                  start=True, stop=False)
                        pe.matmul(pH[r1 % 3][:, :], rT_hi[r1 % 3][:, :], W1_lo[l][:, bass.ds(ev * F, F)],
                                  start=False, stop=False)
                        pe.matmul(pH[r1 % 3][:, :], rT_lo[r1 % 3][:, :], W1_hi[:, bass.ds(ev * F, F)],
                                  start=False, stop=True).then_inc(s_h, 1)
                    if valid(q, r):
                        pe.wait_ge(s_hb, base + num(q, r) + 1)
                        if has_before(l, q, r, 3):
                            pe.wait_ge(s_hTc, base + num(q, r) - 2)
                        for c in range(FC):
                            ins = pe.transpose(pHT[r % 3][:, c * P:(c + 1) * P], hb[r % 3][:, c * P:(c + 1) * P], ident[:, :])
                        ins.then_inc(s_ht, 1)
                    if valid(q0, rp):
                        ev = expert(-1)
                        pe.wait_ge(s_hTc, base + num(q0, rp) + 1)
                        if has_before(0, q0, rp, 1):
                            pe.wait_ge(s_yb if l == 0 else s_y1, num(q0, rp))
                        for c in range(FC):
                            ins = pe.matmul(pY[:, 0:D], hT[rp % 3][:, c * P:(c + 1) * P],
                                            W2[l][:, bass.ds(ev * F + c * P, P)],
                                            start=(c == 0), stop=(c == FC - 1))
                        ins.then_inc(s_y, 1)
                each_tile(pe, 2, 1, step, with_experts=True)

            attention(0)
            route(0)
            mlp(0)
            attention(1)
            route(1)
            mlp(1)


_INS = ["x", "ctx_1024", "g_xattn", "g_ffn",
        "L0_xattn_Wq", "L0_xattn_bq", "L0_xattn_Wk", "L0_xattn_bk", "L0_xattn_Wv", "L0_xattn_bv",
        "L0_ffn_centroids", "L0_ffn_ln_g", "L0_ffn_ln_b", "L0_ffn_w1", "L0_ffn_b1", "L0_ffn_w2", "L0_ffn_b2",
        "L1_xattn_Wq", "L1_xattn_bq", "L1_xattn_Wk", "L1_xattn_bk", "L1_xattn_Wv", "L1_xattn_bv",
        "L1_ffn_wg_red", "L1_ffn_wg", "L1_ffn_w1", "L1_ffn_b1", "L1_ffn_w2", "L1_ffn_b2"]


def kernel(**inputs):
    import numpy as _np
    import concourse.bacc as _bacc
    from concourse import mybir as _mybir
    from concourse.bass_utils import run_bass_kernel_spmd as _run

    nc = _bacc.Bacc("TRN2", target_bir_lowering=False, num_devices=1)
    arrays, args = {}, {}
    for name in _INS:
        a = _np.ascontiguousarray(inputs[name])
        arrays[f"in_{name}_dram"] = a
        args[name] = nc.dram_tensor(f"in_{name}_dram", a.shape, _mybir.dt.from_np(a.dtype), kind="ExternalInput").ap()
    out = nc.dram_tensor("out_0_dram", tuple(inputs["x"].shape), _mybir.dt.float32, kind="ExternalOutput").ap()
    build(nc, args, out)
    r = _run(nc, [arrays], core_ids=[0])
    return r.results[0]["out_0_dram"]
```
